# Optimizing a Trainium2 kernel written in Bass

```python
import numpy as np
import jax
import jax.numpy as jnp

def _softmax(x, axis=-1):
    return jax.nn.softmax(x, axis=axis)

def _gelu(x):
    return jax.nn.gelu(x, approximate=True)

def _silu(x):
    return jax.nn.silu(x)

def _sigmoid(x):
    return jax.nn.sigmoid(x)

def _layernorm(x, axis=-1, eps=1e-05):
    m = jnp.mean(x, axis=axis, keepdims=True)
    v = jnp.var(x, axis=axis, keepdims=True)
    return (x - m) / jnp.sqrt(v + eps)

def _scatter_add(tgt, idx, src, axis=0):
    return tgt.at[idx].add(src)

def _segment_sum(src, seg, n):
    return jax.ops.segment_sum(src, seg, n)
kernel_name = 'mk_adaln_d1_jaxref_r8_0e6775'

def setup_inputs(seed: int=0):
    np.random.seed(seed)
    _w = jnp.asarray

    def _L0_attn_setup():
        import jax, jax.numpy as jnp
        import numpy as np
        D_MODEL = 128
        N_HEADS = 16
        N_GROUPS = 4
        CONTEXT_LEN = 64
        D_H = D_MODEL // N_HEADS
        GROUP_SIZE = N_HEADS // N_GROUPS
        B, S = (4, 256)
        key = jax.random.key(seed)
        ks = jax.random.split(key, 9)
        s = 0.02
        return {'x': jax.random.normal(ks[0], (B, S, D_MODEL), dtype=jnp.float32), 'Wq': jax.random.normal(ks[1], (D_MODEL, D_MODEL), dtype=jnp.float32) * s, 'bq': jax.random.normal(ks[2], (D_MODEL,), dtype=jnp.float32) * s, 'Wk': jax.random.normal(ks[3], (D_MODEL, N_GROUPS * D_H), dtype=jnp.float32) * s, 'bk': jax.random.normal(ks[4], (N_GROUPS * D_H,), dtype=jnp.float32) * s, 'Wv': jax.random.normal(ks[5], (D_MODEL, N_GROUPS * D_H), dtype=jnp.float32) * s, 'bv': jax.random.normal(ks[6], (N_GROUPS * D_H,), dtype=jnp.float32) * s, 'Wo': jax.random.normal(ks[7], (D_MODEL, D_MODEL), dtype=jnp.float32) * s, 'bo': jax.random.normal(ks[8], (D_MODEL,), dtype=jnp.float32) * s}
    _L0_attn_in = _L0_attn_setup()

    def _L0_ffn_setup():
        import jax, jax.numpy as jnp
        import numpy as np
        DIM = 128
        DEPTH = 7
        PAR = 8
        N_NODES = 2 ** (DEPTH + 1) - 1
        WIDTH = PAR * N_NODES
        key = jax.random.key(seed)
        k1, k2, k3, k4 = jax.random.split(key, 4)
        init_k = float(np.sqrt(1.0 / DIM))
        init_k2 = float(np.sqrt(1.0 / ((DEPTH + 1) * PAR)))
        oldx = jax.random.normal(k1, (4, 256, DIM), dtype=jnp.float32)
        W_in = jax.random.uniform(k2, (WIDTH, DIM), jnp.float32, -init_k, init_k)
        b_in = jax.random.uniform(k3, (WIDTH,), jnp.float32, -init_k, init_k)
        W_out = jax.random.uniform(k4, (DIM, WIDTH), jnp.float32, -init_k2, init_k2)
        return {'oldx': oldx, 'W_in': W_in, 'b_in': b_in, 'W_out': W_out}
    _L0_ffn_in = _L0_ffn_setup()
    _L0_c = _w((lambda *s: np.random.randn(*s).astype(np.float32) * 0.05)(4, 128))
    _L0_wmod = _w((lambda *s: np.random.randn(*s).astype(np.float32) * 0.05)(128, 6 * 128) * 128 ** (-0.5))
    _d = {'L0_attn_x': _L0_attn_in['x'], 'L0_attn_Wq': _L0_attn_in['Wq'], 'L0_attn_bq': _L0_attn_in['bq'], 'L0_attn_Wk': _L0_attn_in['Wk'], 'L0_attn_bk': _L0_attn_in['bk'], 'L0_attn_Wv': _L0_attn_in['Wv'], 'L0_attn_bv': _L0_attn_in['bv'], 'L0_attn_Wo': _L0_attn_in['Wo'], 'L0_attn_bo': _L0_attn_in['bo'], 'L0_ffn_W_in': _L0_ffn_in['W_in'], 'L0_ffn_b_in': _L0_ffn_in['b_in'], 'L0_ffn_W_out': _L0_ffn_in['W_out'], 'L0_c': _L0_c, 'L0_wmod': _L0_wmod}
    _x0 = _d['L0_attn_x']
    _d['L0_attn_x'] = jax.random.normal(jax.random.fold_in(jax.random.key(seed), 1), (4, 512, 128), dtype=_x0.dtype)
    del _x0
    return _d

def reference(L0_attn_x, L0_attn_Wq, L0_attn_bq, L0_attn_Wk, L0_attn_bk, L0_attn_Wv, L0_attn_bv, L0_attn_Wo, L0_attn_bo, L0_ffn_W_in, L0_ffn_b_in, L0_ffn_W_out, L0_c, L0_wmod):

    def _L0_attn_ref(x, Wq, bq, Wk, bk, Wv, bv, Wo, bo):
        import jax, jax.numpy as jnp
        import numpy as np
        D_MODEL = 128
        N_HEADS = 16
        N_GROUPS = 4
        CONTEXT_LEN = 64
        D_H = D_MODEL // N_HEADS
        GROUP_SIZE = N_HEADS // N_GROUPS
        B, S = (4, 256)
        b, s = (x.shape[0], x.shape[1])
        q = (x @ Wq + bq).reshape(b, s, N_GROUPS, GROUP_SIZE, D_H)
        q = jnp.transpose(q, (0, 2, 3, 1, 4))
        k = jnp.transpose((x @ Wk + bk).reshape(b, s, N_GROUPS, D_H), (0, 2, 1, 3))
        v = jnp.transpose((x @ Wv + bv).reshape(b, s, N_GROUPS, D_H), (0, 2, 1, 3))
        scores = jnp.einsum('bghqd,bgkd->bghqk', q, k) / jnp.sqrt(jnp.float32(D_H))
        i = jnp.arange(s)
        j = jnp.arange(s)
        upper = (i - CONTEXT_LEN)[:, None] >= j[None, :]
        lower = i[:, None] < j[None, :]
        mask = upper | lower
        scores = jnp.where(mask, jnp.float32(-1000000000.0), scores)
        att = jax.nn.softmax(scores, axis=-1)
        out = jnp.einsum('bghqk,bgkd->bghqd', att, v)
        out = jnp.transpose(out, (0, 3, 1, 2, 4)).reshape(b, s, D_MODEL)
        return out @ Wo + bo

    def _L0_ffn_ref(oldx, W_in, b_in, W_out):
        import jax, jax.numpy as jnp
        import numpy as np
        DIM = 128
        DEPTH = 7
        PAR = 8
        N_NODES = 2 ** (DEPTH + 1) - 1
        WIDTH = PAR * N_NODES
        x = oldx.reshape(-1, DIM)
        B = x.shape[0]
        logits = x @ W_in.T + b_in
        decisions = (logits > 0).astype(jnp.int32).reshape(B, PAR, N_NODES)
        acts = jax.nn.silu(logits).reshape(B, PAR, N_NODES)
        current = jnp.zeros((B, PAR), dtype=jnp.int32)
        dmap = jax.nn.one_hot(current, N_NODES, dtype=acts.dtype)
        for d in range(DEPTH):
            cur_platform = 2 ** d - 1
            next_platform = 2 ** (d + 1) - 1
            moves = jnp.take_along_axis(decisions, current[..., None], axis=2)[..., 0]
            current = (current - cur_platform) * 2 + moves + next_platform
            dmap = dmap + jax.nn.one_hot(current, N_NODES, dtype=acts.dtype)
        masked = acts * jax.lax.stop_gradient(dmap)
        out = masked.reshape(B, WIDTH) @ W_out.T
        return out.reshape(oldx.shape)
    x = L0_attn_x
    mod = (_silu(L0_c) @ L0_wmod).reshape(L0_c.shape[0], 6, 1, -1)
    sa, ca, ga, sb, cb, gb = (mod[:, 0], mod[:, 1], mod[:, 2], mod[:, 3], mod[:, 4], mod[:, 5])
    ga = (2 * (ga >= 0) - 1) * jnp.maximum(jnp.abs(ga), 0.25)
    gb = (2 * (gb >= 0) - 1) * jnp.maximum(jnp.abs(gb), 0.25)
    h = _layernorm(x, axis=-1) * (1 + ca) + sa
    x = x + ga * _L0_attn_ref(h, L0_attn_Wq, L0_attn_bq, L0_attn_Wk, L0_attn_bk, L0_attn_Wv, L0_attn_bv, L0_attn_Wo, L0_attn_bo)
    h = _layernorm(x, axis=-1) * (1 + cb) + sb
    x = x + gb * _L0_ffn_ref(h, L0_ffn_W_in, L0_ffn_b_in, L0_ffn_W_out)
    return x

_drawn_inputs = setup_inputs


def setup_inputs(seed=0):
    import zlib

    import numpy as np

    out = dict(_drawn_inputs(seed))
    spreads = {}
    factors = {'L0_attn_Wq': 8.0,
     'L0_attn_bq': 8.0,
     'L0_attn_Wk': 8.0,
     'L0_attn_bk': 8.0,
     'L0_attn_Wv': 8.0,
     'L0_attn_bv': 8.0,
     'L0_attn_Wo': 8.0,
     'L0_attn_bo': 8.0,
     'L0_ffn_b_in': 3.303}
    for name, (base, spread) in spreads.items():
        noise = np.random.default_rng([zlib.crc32(name.encode()), seed]).standard_normal(out[name].shape)
        drawn = base * np.exp(spread * noise) if base else spread * noise
        out[name] = jnp.asarray(drawn.astype(out[name].dtype))
    for name, factor in factors.items():
        out[name] = (out[name] * factor).astype(out[name].dtype)
    return out
```

```python
from contextlib import ExitStack

import concourse.bass as bass
from concourse import mybir

F32 = mybir.dt.float32
F32R = mybir.dt.float32r
BF16 = mybir.dt.bfloat16
ALU = mybir.AluOpType
ACT = mybir.ActivationFunctionType
AX = mybir.AxisListType

P = 128
D = 128
B, S = 4, 512
NT = S // P
G, HG, DH = 4, 4, 8
NH = G * HG
CONTEXT = 64
QB = 32
NQ = S // QB
WIN = CONTEXT + QB
PAD = CONTEXT
SCALE = DH ** -0.5
EPS = 1e-5

PAR, DEPTH = 8, 7
INNER = 2 ** DEPTH - 1
NODES = 2 ** (DEPTH + 1) - 1
BIG = 2.0 ** 80

RUNS = (3, 2, 1)
MASK_ROW = sum(RUNS) * DH
SHIFT_ROW = MASK_ROW + QB
SCORE_ROWS = 96
PHASES = 3
VW = G * DH
PV_ROWS = 2 * VW
QUAD = 4
NQUAD = NQ // QUAD

LN1_T, Q_PROJ, K_PROJ, ROWS = 0, 1, 2, 3
MAX_T = ROWS + NQ
COLS = MAX_T + 1
OUT_PROJ = COLS + NQ
LN2_T = OUT_PROJ + 1
STEPS = LN2_T + 1
SPLIT = {Q_PROJ: 1, K_PROJ: 2, MAX_T: 3}
assert STEPS % 2 == 0


def reads(bank, step):
    return sum(n % 2 == bank and n not in SPLIT and n != OUT_PROJ for n in range(step))


NP = 3
EXPS_AFTER = 6
GATES = 6
LN_STEPS = 2 * NT + 1


def rows_of_turn(s):
    n = EXPS_AFTER - 3
    return range(NQ * (s - 3) // n, NQ * (s - 2) // n)


def block_program(nc, x, wq, bq, wk, bk, wv, bv, wo, bo, w_in, b_in, w_out, c_t, wmod,
                  q_const, k_const, tree_in, ident_in, out):
    with ExitStack() as ctx:
        def sb(name, shape, dt=F32):
            return ctx.enter_context(nc.sbuf_tensor(name, shape, dt))

        def psum(name, shape):
            return ctx.enter_context(nc.psum_tensor(name, shape, F32))

        def sem(name):
            return ctx.enter_context(nc.semaphore(name))

        wq_sb, wk_sb, wv_sb = sb("wq_sb", [P, D]), sb("wk_sb", [P, P]), sb("wv_sb", [P, G * DH])
        wo_sb = sb("wo_sb", [P, D])
        bq_sb, bk_sb = sb("bq_sb", [P, 1]), sb("bk_sb", [P, 1])
        bv_sb, bo_sb = sb("bv_sb", [WIN, G * DH]), sb("bo_sb", [P, D])
        w_in_sb = sb("w_in_sb", [P, 2 * PAR, P])
        w_out_sb = sb("w_out_sb", [P, 2 * PAR, D])
        b_in_sb = sb("b_in_sb", [P, 2 * PAR])
        c_sb, wmod_sb = sb("c_sb", [P, B]), sb("wmod_sb", [P, 6 * D])
        w_in_hi = sb("w_in_hi", [P, 2 * PAR, P], F32R)
        w_in_lo = sb("w_in_lo", [P, 2 * PAR, P], F32R)
        tree = sb("tree", [P, 2, P], BF16)
        ident = sb("ident", [P, P])
        silu_c = sb("silu_c", [P, B])
        mod = sb("mod", [P, 5, B])
        gate_sign, gate_size = sb("gate_sign", [P, B, D]), sb("gate_size", [P, B, D])
        ga = sb("ga", [P, B, D])
        gb_sign, gb_size = sb("gb_sign", [P, B]), sb("gb_size", [P, B])
        wo_ga, bo_ga = sb("wo_ga", [P, B, D]), sb("bo_ga", [P, B, D])
        x_sb = sb("x_sb", [P, NT, D])
        xb = sb("xb", [P, NT, D])
        stats = sb("stats", [P, 2, NT, 6])
        moments = sb("moments", [P, 2, NT, 2])
        var_eps = sb("var_eps", [P, 2, NT])
        rstd = sb("rstd", [P, 2, NT])
        minus_half = sb("minus_half", [P, NT])
        xn = sb("xn", [P, 2, NT, D])
        h1 = sb("h1", [P, PAD + S])
        q_first, q_second, q_third = (sb(f"q_{n}", [P, S], BF16) for n in ("first", "second", "third"))
        q_rest = sb("q_rest", [P, S])
        k_first, k_second, k_third = (sb(f"k_{n}", [P, S], BF16) for n in ("first", "second", "third"))
        k_rest = sb("k_rest", [P, S])
        q_part = sb("q_part", [3 * VW, NQ, HG, QB], BF16)
        q_stack = sb("q_stack", [SCORE_ROWS, G, NQ, HG * QB], BF16)
        k_stack = sb("k_stack", [SCORE_ROWS, PHASES, G, PAD + S], BF16)
        v_win = sb("v_win", [WIN, NQ, G * (2 * VW + DH)])
        neg_max = sb("neg_max", [P, P])
        max_part = sb("max_part", [2 * G * NQ, P], BF16)
        probs = sb("probs", [WIN, NP, G * P])
        pv = sb("pv", [P, S])
        den = sb("den", [P, S])
        inv_den = sb("inv_den", [P, S])
        attn = sb("attn", [P, S])
        x1 = sb("x1", [P, NT, D])
        h2 = sb("h2", [P, S])
        h2_hi, h2_lo = sb("h2_hi", [P, S], F32R), sb("h2_lo", [P, S], F32R)
        x1_kept = sb("x1_kept", [P, NT, D])
        decided = sb("decided", [P, 2, S], BF16)
        acts = sb("acts", [P, 2, 2, S])
        y_t = sb("y_t", [P, S])
        y = sb("y", [P, NT, D])

        turn_bank = [psum(f"turn_bank{i}", [P, 512]) for i in range(2)]
        pv_bank = psum("pv_bank", [P, 512])
        inner_bank = [psum(f"inner_bank{i}", [P, 512]) for i in range(2)]
        leaf_bank = [psum(f"leaf_bank{i}", [P, 512]) for i in range(2)]
        sum_bank = psum("sum_bank", [P, 512])

        small_loaded, consts_loaded = sem("small_loaded"), sem("consts_loaded")
        attn_w_loaded, mlp_w_loaded = sem("attn_w_loaded"), sem("mlp_w_loaded")
        filled_once = sem("filled_once")
        filled_by_pool = sem("filled_by_pool")
        silu_c_ready, mod_ready = sem("silu_c_ready"), sem("mod_ready")
        mod_sb_ready, gate_steps = sem("mod_sb_ready"), sem("gate_steps")
        x_loaded, xb_ready = sem("x_loaded"), sem("xb_ready")
        ln_steps, rstd_ready, xn_ready = sem("ln_steps"), sem("rstd_ready"), sem("xn_ready")
        bank_filled = sem("bank_filled")
        bank_read = [sem(f"bank_read{i}") for i in range(2)]
        first_ready, rest_ready = sem("first_ready"), sem("rest_ready")
        second_ready, third_ready = sem("second_ready"), sem("third_ready")
        first_placed, later_placed = sem("first_placed"), sem("later_placed")
        q_stacked, k_stacked, phases_ready = sem("q_stacked"), sem("k_stacked"), sem("phases_ready")
        shift_loaded = sem("shift_loaded")
        v_filled, v_ready = sem("v_filled"), sem("v_ready")
        pv_done, den_ready, pv_ready = sem("pv_done"), sem("den_ready"), sem("pv_ready")
        inv_ready, attn_ready, x1_ready = sem("inv_ready"), sem("attn_ready"), sem("x1_ready")
        h2_hi_ready, h2_lo_ready, w_in_split = sem("h2_hi_ready"), sem("h2_lo_ready"), sem("w_in_split")
        x1_kept_ready = sem("x1_kept_ready")
        logits_done, decided_ready = sem("logits_done"), sem("decided_ready")
        masked, acts_ready, summed = sem("masked"), sem("acts_ready"), sem("summed")
        y_t_ready, y_turned = sem("y_t_ready"), sem("y_turned")
        y_ready, y_stored = sem("y_ready"), sem("y_stored")

        STACK_DMAS = 16 * len(RUNS)
        N_SMALL, N_CONST, N_ATTN_W, N_MLP_W = 16 * 3, 16 * 2, 16 * 8, 16 * 4

        def wait(eng, s, per, n, k):
            k = max(k, 0)
            if isinstance(n, int) and n * per + k == 0:
                return
            eng.wait_ge(s, n * per + k)

        def wait_read(eng, a, step):
            if step in SPLIT:
                wait(eng, rest_ready, len(SPLIT), a, SPLIT[step])
            elif step == OUT_PROJ:
                wait(eng, x1_ready, 1, a, 1)
            else:
                wait(eng, bank_read[step % 2], reads(step % 2, STEPS), a, reads(step % 2, step + 1))

        def wait_free(eng, a, step):
            if step >= 2:
                wait_read(eng, a, step - 2)
            else:
                if step % 2 == OUT_PROJ % 2:
                    wait(eng, x1_ready, 1, a, 0)
                wait(eng, bank_read[step % 2], reads(step % 2, STEPS), a, 0)

        def wait_filled(eng, a, step):
            wait(eng, bank_filled, STEPS, a, step + 1)

        def col(n):
            return bass.ds(n, 1) if not isinstance(n, int) else slice(n, n + 1)

        x_tiles = x.rearrange("b (t p) d -> b p t d", p=P)
        out_tiles = out.rearrange("b (t p) d -> b p t d", p=P)

        def by_head(ap, rows, h, blocks):
            return ap[rows, :].rearrange("p (b h q) -> p b h q", h=HG, q=QB)[:, 0:blocks, h, :]

        v_groups = v_win[:, :, :].rearrange("p b (g c) -> p b g c", g=G)

        block = ctx.enter_context(nc.Block())

        @block.sync
        def _(sp):
            sp.dma_start(c_sb[:, :], c_t).then_inc(small_loaded, 16)
            sp.dma_start(wmod_sb[:, :], wmod).then_inc(small_loaded, 16)
            sp.dma_start(ident[:, :], ident_in).then_inc(small_loaded, 16)
            sp.dma_start(wq_sb[:, :], wq).then_inc(attn_w_loaded, 16)
            sp.dma_start(bq_sb[:, :], bq).then_inc(attn_w_loaded, 16)
            sp.dma_start(wk_sb[:, :], wk).then_inc(attn_w_loaded, 16)
            sp.dma_start(bk_sb[:, :], bk).then_inc(attn_w_loaded, 16)
            sp.dma_start(wv_sb[:, :], wv).then_inc(attn_w_loaded, 16)
            sp.dma_start(bv_sb[:, :], bv).then_inc(attn_w_loaded, 16)
            sp.dma_start(wo_sb[:, :], wo).then_inc(attn_w_loaded, 16)
            sp.dma_start(bo_sb[:, :], bo).then_inc(attn_w_loaded, 16)
            sp.dma_start(tree[:, :, :], tree_in.bitcast(BF16)).then_inc(mlp_w_loaded, 16)

            def stack_q_and_k(a, before):
                if before is not None:
                    wait_filled(sp, before, COLS + NQ - 1)
                row = MASK_ROW
                for run, k_part, ready, n in ((1, k_third, third_ready, 2), (2, k_second, second_ready, 2),
                                              (3, k_first, first_ready, 2)):
                    row -= run * DH
                    if run == 1:
                        wait(sp, first_placed, HG, a, HG)
                    else:
                        wait(sp, later_placed, 2 * HG, a, (run - 1) * HG)
                    sp.dma_start(q_stack[row:row + run * DH, :, :, :].rearrange("p g b c -> p g (b c)"),
                                 q_part[0:run * VW, :, :, :].rearrange("p b h q -> p (b h q)"))\
                        .then_inc(q_stacked, 16)
                    wait(sp, ready, (len(SPLIT) if run == 3 else 2), a, n)
                    sp.dma_start(k_stack[row:row + run * DH, 0, :, PAD:], k_part[0:run * VW, :])\
                        .then_inc(k_stacked, 16)

            def stack_max(a):
                wait(sp, first_ready, len(SPLIT), a, len(SPLIT))
                wait(sp, rest_ready, len(SPLIT), a, len(SPLIT))
                sp.dma_start(q_stack[SHIFT_ROW:SHIFT_ROW + 2, :, :, :].rearrange("p g b c -> p (g b) c"),
                             max_part[:, :]).then_inc(shift_loaded, 16)

            sp.wait_ge(consts_loaded, N_CONST)
            stack_q_and_k(0, None)
            stack_max(0)
            with sp.Fori(0, B - 1) as i:
                stack_q_and_k(i + 1, i)
                stack_max(i + 1)

        @block.gpsimd
        def _(pool):
            def load_x(n, a):
                if a is not None:
                    wait(pool, xn_ready, 2, a, 1)
                    wait(pool, xb_ready, 1, a, 1)
                pool.dma_start(x_sb[:, :, :], x_tiles[n]).then_inc(x_loaded, 16)

            def store(f):
                wait(pool, y_ready, 1, f, 1)
                pool.dma_start(out_tiles[f], y[:, :, :]).then_inc(y_stored, 16)
                wait(pool, y_stored, 16, f, 1 * 16)

            def inverse_deviation(n, a):
                wait(pool, ln_steps, 2 * LN_STEPS, a, (n + 1) * LN_STEPS)
                pool.tensor_tensor(rstd[:, n, :], var_eps[:, n, :], minus_half[:, :], ALU.pow)\
                    .then_inc(rstd_ready, 1)

            load_x(0, None)
            pool.memset(minus_half[:, :], -0.5).then_inc(filled_by_pool, 1)
            pool.wait_ge(filled_by_pool, 1)
            inverse_deviation(0, 0)
            load_x(1, 0)
            pool.wait_ge(mlp_w_loaded, N_MLP_W)
            for t in range(0, 2 * PAR, 4):
                pool.tensor_copy(w_in_hi[:, t:t + 4, :], w_in_sb[:, t:t + 4, :]).then_inc(w_in_split, 1)
            for t in range(0, 2 * PAR, 4):
                pool.wait_ge(w_in_split, t // 4 + 1)
                pool.tensor_tensor(w_in_lo[:, t:t + 4, :], w_in_sb[:, t:t + 4, :],
                                   w_in_hi[:, t:t + 4, :].bitcast(F32), ALU.subtract).then_inc(w_in_split, 1)
            inverse_deviation(1, 0)
            with pool.Fori(0, B - 2) as i:
                inverse_deviation(0, i + 1)
                load_x(i + 2, i + 1)
                inverse_deviation(1, i + 1)
                store(i)
            inverse_deviation(0, B - 1)
            inverse_deviation(1, B - 1)
            store(B - 2)
            store(B - 1)

        @block.scalar
        def _(act):
            act.dma_start(q_stack[MASK_ROW:, :, :, :].rearrange("p g b c -> p g (b c)"),
                          q_const.bitcast(BF16).rearrange("p (g c) -> p g c", g=1).to_broadcast([SCORE_ROWS - MASK_ROW, G, HG * S]))\
                .then_inc(consts_loaded, 16)
            act.dma_start(k_stack[MASK_ROW:, :, :, :].rearrange("p f g c -> p (f g) c"), k_const.bitcast(BF16))\
                .then_inc(consts_loaded, 16)
            act.dma_start(w_in_sb[:, :, :], w_in).then_inc(mlp_w_loaded, 16)
            act.dma_start(w_out_sb[:, :, :], w_out).then_inc(mlp_w_loaded, 16)
            act.dma_start(b_in_sb[:, :], b_in).then_inc(mlp_w_loaded, 16)
            act.wait_ge(small_loaded, N_SMALL)
            nc.scalar.activation(silu_c[:, :], c_sb[:, :], ACT.Silu).then_inc(silu_c_ready, 1)

            def project(a):
                if isinstance(a, int) and a == 0:
                    act.wait_ge(mod_sb_ready, 1)
                    act.wait_ge(filled_once, 1)
                    act.wait_ge(attn_w_loaded, N_ATTN_W)
                wait_filled(act, a, LN1_T)
                nc.scalar.activation(h1[:, PAD:], turn_bank[LN1_T % 2][:, :], ACT.Identity,
                                     bias=mod[:, 0, col(a)], scale=mod[:, 1, col(a)])\
                    .then_inc(bank_read[LN1_T % 2], 1)
                wait(act, q_stacked, STACK_DMAS, a, 0)
                wait(act, k_stacked, STACK_DMAS, a, 0)
                wait_filled(act, a, Q_PROJ)
                nc.scalar.activation(q_first[:, :], turn_bank[Q_PROJ % 2][:, :], ACT.Identity,
                                     bias=bq_sb[:, :]).then_inc(first_ready, 1)
                wait_filled(act, a, K_PROJ)
                nc.scalar.activation(k_first[:, :], turn_bank[K_PROJ % 2][:, :], ACT.Identity,
                                     bias=bk_sb[:, :]).then_inc(first_ready, 1)
                wait(act, first_ready, len(SPLIT), a, 1)
                for h in range(HG):
                    nc.scalar.activation(q_part[0:VW, :, h, :],
                                         q_first[h * VW:(h + 1) * VW, :].rearrange("p (b q) -> p b q", q=QB),
                                         ACT.Identity).then_inc(first_placed, 1)

            def round_max(a):
                wait_filled(act, a, MAX_T)
                wait(act, shift_loaded, 16, a, 0)
                nc.scalar.activation(max_part[0:G * NQ, :], turn_bank[MAX_T % 2][0:G * NQ, 0:P],
                                     ACT.Identity).then_inc(first_ready, 1)

            def exps(a):
                for b in range(NQ):
                    step = COLS + b
                    wait_filled(act, a, step)
                    wait(act, pv_done, NQ, a, b - NP + 1)
                    nc.scalar.activation(probs[:, b % NP, :], turn_bank[step % 2][0:WIN, :], ACT.Exp,
                                         scale=SCALE).then_inc(bank_read[step % 2], 1)
                    if b % QUAD == 1 and b > QUAD:
                        sums(a, b // QUAD - 1)
                sums(a, NQUAD - 1)

            def sums(a, n):
                wait(act, pv_done, NQ, a, (n + 1) * QUAD)
                top = (n % 2) * PV_ROWS + VW
                for h in range(HG):
                    ins = nc.scalar.activation(
                        den[h * VW:(h + 1) * VW, n * P:(n + 1) * P].rearrange("p (b q) -> p b q", q=QB),
                        by_head(pv_bank, slice(top, top + VW), h, QUAD), ACT.Identity)
                ins.then_inc(den_ready, 1)

            def second_h(a):
                wait_filled(act, a, LN2_T)
                if not (isinstance(a, int) and a == 0):
                    wait(act, logits_done, 2 * PAR, a, 0)
                for h, done in ((h2_hi, h2_hi_ready), (h2, bank_read[LN2_T % 2])):
                    nc.scalar.activation(h[:, :], turn_bank[LN2_T % 2][:, :], ACT.Identity,
                                         bias=mod[:, 2, col(a)], scale=mod[:, 3, col(a)]).then_inc(done, 1)

            def silus(t, f):
                for n, bank in enumerate((inner_bank, leaf_bank)):
                    wait(act, masked, 2 * PAR, f, 2 * t + n + 1)
                    if t >= 2:
                        wait(act, summed, PAR, f, t - 1)
                    nc.scalar.activation(acts[:, t % 2, n, :], bank[t % 2][:, :], ACT.Silu,
                                         bias=b_in_sb[:, 2 * t + n:2 * t + n + 1])\
                        .then_inc(acts_ready, 1)

            project(0)
            round_max(0)
            exps(0)
            second_h(0)
            act.wait_ge(mlp_w_loaded, N_MLP_W)
            with act.Fori(0, B - 1) as i:
                project(i + 1)
                for t in range(EXPS_AFTER - 1):
                    silus(t, i)
                round_max(i + 1)
                silus(EXPS_AFTER - 1, i)
                exps(i + 1)
                silus(EXPS_AFTER, i)
                silus(EXPS_AFTER + 1, i)
                second_h(i + 1)
            for t in range(PAR):
                silus(t, B - 1)

        @block.vector
        def _(dve):
            dve.memset(h1[:, 0:PAD], 0.0)
            dve.memset(neg_max[:, G * NQ:], 0.0)
            dve.memset(k_stack[0:MASK_ROW, :, :, 0:PAD], 0.0)
            dve.memset(v_win[:, :, :], 0.0).then_inc(filled_once, 1)
            dve.wait_ge(filled_once, 1)
            dve.memset(v_groups[:, :, :, VW:VW + DH], 1.0).then_inc(filled_once, 1)

            def token_stats(n, src):
                for t in range(NT):
                    dve.bn_stats(stats[:, n, t, :], src[:, t, :]).then_inc(ln_steps, 1)

            def wait_token_stats(n, a):
                wait(dve, ln_steps, 2 * LN_STEPS, a, n * LN_STEPS + NT)

            def moments_of(n, a):
                for t in range(NT):
                    dve.bn_aggr(moments[:, n, t, :], stats[:, n, t, :]).then_inc(ln_steps, 1)
                wait(dve, ln_steps, 2 * LN_STEPS, a, n * LN_STEPS + 2 * NT)
                dve.tensor_scalar(var_eps[:, n, :], moments[:, n, :, 1], EPS, None, ALU.add)\
                    .then_inc(ln_steps, 1)

            def attention_bias(a):
                if not (isinstance(a, int) and a == 0):
                    wait(dve, x1_ready, 1, a, 0)
                dve.tensor_tensor(xb[:, :, :], x_sb[:, :, :],
                                  bo_ga[:, col(a), :].to_broadcast([P, NT, D]), ALU.add)\
                    .then_inc(xb_ready, 1)

            def normalize(n, a, src):
                wait(dve, rstd_ready, 2, a, n + 1)
                if n == 0:
                    wait(dve, bank_filled, STEPS, a, 0)
                for t in range(NT):
                    ins = dve.tensor_scalar(xn[:, n, t, :], src[:, t, :], moments[:, n, t, 0:1],
                                            rstd[:, n, t:t + 1], ALU.subtract, ALU.mult)
                ins.then_inc(xn_ready, 1)

            def split_parts(a):
                wait(dve, q_stacked, STACK_DMAS, a, 0)
                wait(dve, k_stacked, STACK_DMAS, a, 0)
                sides = ((turn_bank[Q_PROJ % 2], bq_sb, q_first, q_rest, q_second, q_third),
                         (turn_bank[K_PROJ % 2], bk_sb, k_first, k_rest, k_second, k_third))
                for n, (bank, bias, first, rest, second, third) in enumerate(sides):
                    wait(dve, first_ready, len(SPLIT), a, n + 1)
                    dve.scalar_tensor_tensor(out=rest[:, :], in0=bank[:, :], scalar=bias[:, :], in1=first[:, :],
                                             op0=ALU.add, op1=ALU.subtract).then_inc(rest_ready, 1)
                for n, (bank, bias, first, rest, second, third) in enumerate(sides):
                    wait(dve, rest_ready, len(SPLIT), a, n + 1)
                    dve.tensor_copy(second[:, :], rest[:, :]).then_inc(second_ready, 1)
                for n, (bank, bias, first, rest, second, third) in enumerate(sides):
                    wait(dve, second_ready, 2, a, n + 1)
                    dve.tensor_tensor(third[:, :], rest[:, :], second[:, :], ALU.subtract).then_inc(third_ready, 1)

            def place_heads(a):
                for n, part in ((1, q_second), (2, q_third)):
                    if n == 2:
                        wait(dve, third_ready, 2, a, 1)
                    for h in range(HG):
                        dve.tensor_copy(q_part[n * VW:(n + 1) * VW, :, h, :],
                                        part[h * VW:(h + 1) * VW, :].rearrange("p (b q) -> p b q", q=QB))\
                            .then_inc(later_placed, 1)

            def phases(a):
                wait(dve, k_stacked, STACK_DMAS, a, STACK_DMAS)
                for n in range(1, PHASES):
                    dve.tensor_copy(k_stack[0:MASK_ROW, n, :, PAD:], k_stack[0:MASK_ROW, 0, :, PAD:])\
                        .then_inc(phases_ready, 1)

            def values(a):
                wait(dve, v_filled, 1, a, 1)
                dve.tensor_tensor(
                    v_groups[:, :, :, 0:DH],
                    pv_bank[0:WIN, :].rearrange("p (b g d) -> p b g d", g=G, d=DH),
                    bv_sb[:, None, :].rearrange("p o (g d) -> p o g d", g=G)
                    .to_broadcast([WIN, NQ, G, DH]), ALU.add).then_inc(v_ready, 1)

            def row_max(a, b):
                wait_filled(dve, a, ROWS + b)
                dve.tensor_reduce(neg_max[:, b:G * NQ:NQ],
                                  turn_bank[(ROWS + b) % 2][:, 0:G * WIN].rearrange("p (g k) -> p g k", g=G),
                                  AX.X, ALU.max, negate=True).then_inc(bank_read[(ROWS + b) % 2], 1)

            def max_low_part(a):
                wait_filled(dve, a, MAX_T)
                wait(dve, first_ready, len(SPLIT), a, SPLIT[MAX_T])
                wait(dve, shift_loaded, 16, a, 0)
                dve.tensor_tensor(max_part[G * NQ:, :], turn_bank[MAX_T % 2][0:G * NQ, 0:P],
                                  max_part[0:G * NQ, :], ALU.subtract).then_inc(rest_ready, 1)

            def products(a, n):
                wait(dve, pv_done, NQ, a, (n + 1) * QUAD)
                top = (n % 2) * PV_ROWS
                for h in range(HG):
                    ins = dve.tensor_copy(
                        pv[h * VW:(h + 1) * VW, n * P:(n + 1) * P].rearrange("p (b q) -> p b q", q=QB),
                        by_head(pv_bank, slice(top, top + VW), h, QUAD))
                ins.then_inc(pv_ready, 1)

            def divide(a, half):
                n = (half + 1) * NQUAD // 2
                own = slice(half * S // 2, (half + 1) * S // 2)
                wait(dve, den_ready, NQUAD, a, n)
                dve.reciprocal(inv_den[:, own], den[:, own]).then_inc(inv_ready, 1)
                wait(dve, pv_ready, NQUAD, a, n)
                wait(dve, inv_ready, 2, a, half + 1)
                dve.tensor_tensor(attn[:, own], pv[:, own], inv_den[:, own], ALU.mult).then_inc(attn_ready, 1)

            def outputs(a):
                products(a, 0)
                products(a, 1)
                divide(a, 0)
                products(a, 2)
                products(a, 3)
                divide(a, 1)

            def h2_low_part(a):
                wait_read(dve, a, LN2_T)
                dve.tensor_tensor(h2_lo[:, :], h2[:, :], h2_hi[:, :].bitcast(F32), ALU.subtract)\
                    .then_inc(h2_lo_ready, 1)

            def first_residual(a):
                wait_filled(dve, a, OUT_PROJ)
                wait(dve, xb_ready, 1, a, 1)
                wait(dve, x1_kept_ready, 1, a, 0)
                dve.tensor_tensor(x1[:, :, :], turn_bank[OUT_PROJ % 2][:, :].rearrange("p (t d) -> p t d", d=D),
                                  xb[:, :, :], ALU.add).then_inc(x1_ready, 1)

            def keep_x1(a):
                dve.tensor_copy(x1_kept[:, :, :], x1[:, :, :]).then_inc(x1_kept_ready, 1)

            def decisions(t, f):
                wait(dve, logits_done, 2 * PAR, f, 2 * t + 1)
                if t >= 2:
                    wait(dve, masked, 2 * PAR, f, 2 * t - 2)
                dve.tensor_scalar(decided[:, t % 2, :], inner_bank[t % 2][:, :],
                                  b_in_sb[:, 2 * t:2 * t + 1], 0.0, ALU.add, ALU.is_gt)\
                    .then_inc(decided_ready, 1)

            def scale_sum(f):
                wait(dve, summed, PAR, f, PAR)
                dve.tensor_scalar(y_t[:, :], sum_bank[:, :], mod[:, 4, col(f)], None, ALU.mult)\
                    .then_inc(y_t_ready, 1)

            def second_residual(f):
                wait(dve, y_turned, 1, f, 1)
                wait(dve, x1_kept_ready, 1, f, 1)
                if isinstance(f, int):
                    wait(dve, y_stored, 16, f, 0)
                dve.tensor_tensor(y[:, :, :], sum_bank[:, :].rearrange("p (t d) -> p t d", d=D),
                                  x1_kept[:, :, :], ALU.add).then_inc(y_ready, 1)

            def signed_size(sign, size, gate, src, done, n):
                dve.tensor_scalar(sign, src, 0.0, 2.0, ALU.is_ge, ALU.mult).then_inc(done, 1)
                dve.wait_ge(done, n + 1)
                dve.scalar_tensor_tensor(out=size, in0=sign, scalar=-1.0, in1=src,
                                         op0=ALU.add, op1=ALU.mult).then_inc(done, 1)
                dve.wait_ge(done, n + 2)
                dve.tensor_scalar(size, size, 0.25, None, ALU.max).then_inc(done, 1)
                dve.wait_ge(done, n + 3)
                dve.scalar_tensor_tensor(out=gate, in0=sign, scalar=-1.0, in1=size,
                                         op0=ALU.add, op1=ALU.mult).then_inc(done, 1)

            def gates():
                dve.wait_ge(mod_ready, 1)
                m = pv_bank[:, 0:5 * B].rearrange("p (j b) -> p j b", b=B)
                dve.tensor_copy(mod[:, 0:3:2, :], m[:, 0:3:2, :])
                dve.tensor_scalar(mod[:, 1:4:2, :], m[:, 1:4:2, :], 1.0, None, ALU.add).then_inc(mod_sb_ready, 1)
                signed_size(gb_sign[:, :], gb_size[:, :], mod[:, 4, :], m[:, 4, :], mod_sb_ready, 1)

            def output_gates():
                dve.wait_ge(mod_ready, 2)
                m = sum_bank[:, :].rearrange("p (b d) -> p b d", d=D)
                signed_size(gate_sign[:, :, :], gate_size[:, :, :], ga[:, :, :], m, gate_steps, 0)
                dve.wait_ge(gate_steps, 4)
                dve.wait_ge(attn_w_loaded, N_ATTN_W)
                for src, dst in ((wo_sb, wo_ga), (bo_sb, bo_ga)):
                    dve.tensor_tensor(dst[:, :, :], src[:, None, :].to_broadcast([P, B, D]), ga[:, :, :],
                                      ALU.mult).then_inc(gate_steps, 1)

            dve.wait_ge(x_loaded, 16)
            token_stats(0, x_sb)
            wait_token_stats(0, 0)
            moments_of(0, 0)
            gates()
            normalize(0, 0, x_sb)
            dve.wait_ge(attn_w_loaded, N_ATTN_W)
            split_parts(0)
            place_heads(0)
            values(0)
            output_gates()
            dve.wait_ge(gate_steps, GATES)
            attention_bias(0)
            phases(0)
            for b in range(NQ):
                row_max(0, b)
            max_low_part(0)
            outputs(0)
            first_residual(0)
            dve.wait_ge(x1_ready, 1)
            token_stats(1, x1)
            wait_token_stats(1, 0)
            moments_of(1, 0)
            normalize(1, 0, x1)
            keep_x1(0)
            h2_low_part(0)
            dve.wait_ge(mlp_w_loaded, N_MLP_W)

            with dve.Fori(0, B - 1) as i:
                a = i + 1
                wait(dve, x_loaded, 16, a, 16)
                token_stats(0, x_sb)
                wait_token_stats(0, a)
                attention_bias(a)
                moments_of(0, a)
                decisions(0, i)
                normalize(0, a, x_sb)
                decisions(1, i)
                split_parts(a)
                place_heads(a)
                decisions(2, i)
                values(a)
                phases(a)
                for t in range(3, EXPS_AFTER):
                    decisions(t, i)
                    for b in rows_of_turn(t):
                        row_max(a, b)
                max_low_part(a)
                decisions(EXPS_AFTER, i)
                outputs(a)
                decisions(EXPS_AFTER + 1, i)
                first_residual(a)
                wait(dve, x1_ready, 1, a, 1)
                token_stats(1, x1)
                wait_token_stats(1, a)
                scale_sum(i)
                moments_of(1, a)
                normalize(1, a, x1)
                second_residual(i)
                wait(dve, y_ready, 1, i, 1)
                keep_x1(a)
                h2_low_part(a)

            for t in range(PAR):
                decisions(t, B - 1)
            scale_sum(B - 1)
            second_residual(B - 1)

        @block.tensor
        def _(pe):
            def modulation():
                pe.wait_ge(silu_c_ready, 1)
                for j, part in enumerate((0, 1, 3, 4, 5)):
                    ins = pe.matmul(pv_bank[:, j * B:(j + 1) * B], wmod_sb[:, part * D:(part + 1) * D],
                                    silu_c[:, :], start=True, stop=True)
                ins.then_inc(mod_ready, 1)
                for b in range(B):
                    ins = pe.matmul(sum_bank[:, b * D:(b + 1) * D], silu_c[:, b:b + 1].to_broadcast([P, P]),
                                    wmod_sb[:, 2 * D:3 * D], start=True, stop=True)
                ins.then_inc(mod_ready, 1)

            def turn_xn(n, a, step):
                wait(pe, xn_ready, 2, a, n + 1)
                wait_free(pe, a, step)
                for t in range(NT):
                    ins = pe.transpose(turn_bank[step % 2][:, t * P:(t + 1) * P], xn[:, n, t, :], ident[:, :])
                ins.then_inc(bank_filled, 1)

            def project_q_and_k(a):
                wait_read(pe, a, LN1_T)
                wait_free(pe, a, Q_PROJ)
                pe.matmul(turn_bank[Q_PROJ % 2][:, :], wq_sb[:, :], h1[:, PAD:], start=True, stop=True)\
                    .then_inc(bank_filled, 1)
                wait_free(pe, a, K_PROJ)
                pe.matmul(turn_bank[K_PROJ % 2][:, :], wk_sb[:, :], h1[:, PAD:], start=True, stop=True)\
                    .then_inc(bank_filled, 1)

            def project_v(a):
                wait(pe, den_ready, NQUAD, a, 0)
                wait(pe, pv_ready, NQUAD, a, 0)
                for b in range(NQ):
                    ins = pe.matmul(pv_bank[0:WIN, b * VW:(b + 1) * VW],
                                    h1[:, b * QB:b * QB + WIN], wv_sb[:, :], start=True, stop=True)
                ins.then_inc(v_filled, 1)

            def q_block(g, b, rows):
                return q_stack[0:rows, g, b, :]

            def k_window(g, b, rows):
                return k_stack[0:rows, b % PHASES, g, b * QB:b * QB + WIN]

            def score_rows(a, b):
                if b == 0:
                    wait(pe, q_stacked, STACK_DMAS, a, STACK_DMAS)
                    wait(pe, k_stacked, STACK_DMAS, a, STACK_DMAS)
                    wait(pe, phases_ready, PHASES - 1, a, PHASES - 1)
                wait_free(pe, a, ROWS + b)
                for g in range(G):
                    ins = pe.matmul(turn_bank[(ROWS + b) % 2][:, g * WIN:(g + 1) * WIN],
                                    q_block(g, b, SHIFT_ROW), k_window(g, b, SHIFT_ROW),
                                    start=True, stop=True)
                ins.then_inc(bank_filled, 1)

            def turn_max(a):
                wait_read(pe, a, MAX_T - 2)
                wait_read(pe, a, MAX_T - 1)
                pe.transpose(turn_bank[MAX_T % 2][:, 0:P], neg_max[:, :], ident[:, :])\
                    .then_inc(bank_filled, 1)

            def score_cols(a, b):
                if b == 0:
                    wait(pe, shift_loaded, 16, a, 16)
                wait_free(pe, a, COLS + b)
                for g in range(G):
                    ins = pe.matmul(turn_bank[(COLS + b) % 2][0:WIN, g * P:(g + 1) * P],
                                    k_window(g, b, SCORE_ROWS), q_block(g, b, SCORE_ROWS),
                                    start=True, stop=True)
                ins.then_inc(bank_filled, 1)

            def times_v(a, b):
                step = COLS + b
                wait_read(pe, a, step)
                n = b // QUAD
                if b == 0:
                    wait(pe, v_ready, 1, a, 1)
                if n >= 2 and b % QUAD == 0:
                    wait(pe, den_ready, NQUAD, a, n - 1)
                    wait(pe, pv_ready, NQUAD, a, n - 1)
                top = (n % 2) * PV_ROWS
                for g in range(G):
                    ins = pe.matmul(pv_bank[top:top + PV_ROWS, (b % QUAD) * P:(b % QUAD + 1) * P],
                                    v_win[:, b, g * PV_ROWS:(g + 1) * PV_ROWS],
                                    probs[:, b % NP, g * P:(g + 1) * P], start=(g == 0), stop=(g == G - 1))
                ins.then_inc(pv_done, 1)

            def attend(a):
                score_cols(a, 0)
                for b in range(1, NQ):
                    score_cols(a, b)
                    times_v(a, b - 1)
                times_v(a, NQ - 1)

            def project_out(a):
                wait(pe, attn_ready, 2, a, 2)
                wait_free(pe, a, OUT_PROJ)
                for t in range(NT):
                    ins = pe.matmul(turn_bank[OUT_PROJ % 2][:, t * D:(t + 1) * D], attn[:, t * P:(t + 1) * P],
                                    wo_ga[:, col(a), :], start=True, stop=True)
                ins.then_inc(bank_filled, 1)

            def logits(t, f):
                if t == 0:
                    wait_read(pe, f, LN2_T)
                    wait(pe, h2_lo_ready, 1, f, 1)
                for n, bank in enumerate((inner_bank, leaf_bank)):
                    if t >= 2:
                        wait(pe, acts_ready, 2 * PAR, f, 2 * (t - 2) + n + 1)
                    for w, h in ((w_in_hi, h2_hi), (w_in_hi, h2_lo), (w_in_lo, h2_hi)):
                        ins = pe.matmul(bank[t % 2][:, :], w[:, 2 * t + n, :], h[:, :], start=(w is w_in_hi and h is h2_hi),
                                        stop=False, skip_group_check=True)
                    ins.then_inc(logits_done, 1)

            def mask(t, f):
                wait(pe, decided_ready, PAR, f, t + 1)
                for n, bank in enumerate((inner_bank, leaf_bank)):
                    pe.matmul(bank[t % 2][:, :], tree[:, n, :], decided[:, t % 2, :], start=False, stop=True,
                              skip_group_check=True).then_inc(masked, 1)

            def sum_nodes(t, f):
                for n in range(2):
                    wait(pe, acts_ready, 2 * PAR, f, 2 * t + n + 1)
                    ins = pe.matmul(sum_bank[:, :], w_out_sb[:, 2 * t + n, :], acts[:, t % 2, n, :],
                                    start=(t + n == 0), stop=(t == PAR - 1 and n == 1))
                ins.then_inc(summed, 1)

            def turn_sum(f):
                wait(pe, y_t_ready, 1, f, 1)
                for t in range(NT):
                    ins = pe.transpose(sum_bank[:, t * P:(t + 1) * P], y_t[:, t * P:(t + 1) * P], ident[:, :])
                ins.then_inc(y_turned, 1)

            def tree_turn(s, f):
                if s < PAR:
                    logits(s, f)
                if 1 <= s <= PAR:
                    mask(s - 1, f)
                if s >= 2:
                    sum_nodes(s - 2, f)

            pe.wait_ge(small_loaded, N_SMALL)
            modulation()
            turn_xn(0, 0, LN1_T)
            pe.wait_ge(attn_w_loaded, N_ATTN_W)
            project_q_and_k(0)
            project_v(0)
            pe.wait_ge(consts_loaded, N_CONST)
            pe.wait_ge(filled_once, 2)
            for b in range(NQ):
                score_rows(0, b)
            turn_max(0)
            attend(0)
            pe.wait_ge(gate_steps, GATES)
            project_out(0)
            turn_xn(1, 0, LN2_T)
            pe.wait_ge(mlp_w_loaded, N_MLP_W)
            pe.wait_ge(w_in_split, 2 * PAR // 2)

            with pe.Fori(0, B - 1) as i:
                a = i + 1
                tree_turn(0, i)
                turn_xn(0, a, LN1_T)
                tree_turn(1, i)
                project_q_and_k(a)
                tree_turn(2, i)
                project_v(a)
                for s in range(3, EXPS_AFTER):
                    tree_turn(s, i)
                    for b in rows_of_turn(s):
                        score_rows(a, b)
                turn_max(a)
                tree_turn(EXPS_AFTER, i)
                attend(a)
                tree_turn(EXPS_AFTER + 1, i)
                tree_turn(PAR, i)
                project_out(a)
                tree_turn(PAR + 1, i)
                turn_xn(1, a, LN2_T)
                turn_sum(i)

            for s in range(PAR + 2):
                tree_turn(s, B - 1)
            turn_sum(B - 1)


def as_bf16(constants):
    import numpy as np
    return (constants.view(np.uint32) >> 16).astype(np.uint16)


def mask_rows():
    import numpy as np
    q = np.zeros((SCORE_ROWS - MASK_ROW, NQ * HG, QB), np.float32)
    k = np.zeros((SCORE_ROWS - MASK_ROW, PHASES, G, PAD + S), np.float32)
    for i in range(QB):
        q[i, :, i] = 1.0
        for phase in range(PHASES):
            place = (np.arange(PAD + S) - phase * QB) % WIN
            k[i, phase, :, (place <= i) | (place - CONTEXT > i)] = -BIG
    k[:QB, :, :, :PAD] = -BIG
    k[QB:QB + 2] = 1.0
    return as_bf16(q.reshape(-1, HG * S)), as_bf16(k.reshape(-1, PHASES * G, PAD + S))


def tree_matrices():
    import numpy as np
    m = np.zeros((P, 2 * P), np.float32)
    for node in range(NODES):
        at = node if node < INNER else P + node - INNER
        rights = 0
        below = node
        while below:
            above, right = (below - 1) // 2, below % 2 == 0
            m[above, at] = BIG if right else -BIG
            rights += right
            below = above
        m[P - 1, at] = -BIG * rights
    return as_bf16(m.reshape(P, 2, P))


def kernel(L0_attn_x, L0_attn_Wq, L0_attn_bq, L0_attn_Wk, L0_attn_bk, L0_attn_Wv, L0_attn_bv, L0_attn_Wo,
           L0_attn_bo, L0_ffn_W_in, L0_ffn_b_in, L0_ffn_W_out, L0_c, L0_wmod):
    import numpy as np
    import concourse.bacc as bacc
    from concourse.bass_utils import run_bass_kernel_spmd

    f = np.ascontiguousarray
    w_in = np.zeros((PAR, 2 * P, D), np.float32)
    w_out = np.zeros((PAR, 2 * P, D), np.float32)
    b_in = np.ones((PAR, 2 * P), np.float32)
    for dst, src in ((w_in, np.asarray(L0_ffn_W_in).reshape(PAR, NODES, D)),
                     (w_out, np.asarray(L0_ffn_W_out).T.reshape(PAR, NODES, D)),
                     (b_in, np.asarray(L0_ffn_b_in).reshape(PAR, NODES))):
        dst[:, :INNER] = src[:, :INNER]
        dst[:, P:] = src[:, INNER:]
    q_const, k_const = mask_rows()
    wq = np.asarray(L0_attn_Wq).reshape(D, G, HG, DH).transpose(0, 2, 3, 1).reshape(D, D)
    bq = np.asarray(L0_attn_bq).reshape(G, HG, DH).transpose(1, 2, 0).reshape(D, 1)
    wk = np.tile(np.asarray(L0_attn_Wk).reshape(D, G, DH).transpose(0, 2, 1).reshape(D, VW), (1, P // VW))
    bk = np.tile(np.asarray(L0_attn_bk).reshape(G, DH).T.reshape(VW, 1), (P // VW, 1))
    wo = np.asarray(L0_attn_Wo).reshape(G, HG, DH, D).transpose(1, 0, 2, 3).reshape(D, D)
    arrays = {
        "x": f(L0_attn_x), "wq": f(wq), "bq": f(bq),
        "wk": f(wk), "bk": f(bk),
        "wv": f(L0_attn_Wv), "bv": f(np.broadcast_to(np.asarray(L0_attn_bv), (WIN, G * DH))),
        "wo": f(wo), "bo": f(np.broadcast_to(np.asarray(L0_attn_bo), (P, D))),
        "w_in": f(w_in.reshape(2 * PAR, P, D).transpose(2, 0, 1)),
        "b_in": f(b_in.reshape(2 * PAR, P).T),
        "w_out": f(w_out.reshape(2 * PAR, P, D).transpose(1, 0, 2)),
        "c_t": f(np.asarray(L0_c).T), "wmod": f(L0_wmod),
        "q_const": q_const, "k_const": k_const, "tree": tree_matrices(),
        "ident": np.eye(P, dtype=np.float32),
    }
    nc = bacc.Bacc("TRN2", target_bir_lowering=False, num_devices=1)
    args = [nc.dram_tensor(f"in_{n}", a.shape, mybir.dt.from_np(a.dtype), kind="ExternalInput").ap()
            for n, a in arrays.items()]
    out = nc.dram_tensor("out", (B, S, D), F32, kind="ExternalOutput").ap()
    block_program(nc, *args, out)
    r = run_bass_kernel_spmd(nc, [{f"in_{n}": a for n, a in arrays.items()}], core_ids=[0])
    return r.results[0]["out"]
```

```python
from contextlib import ExitStack

import concourse.bass as bass
from concourse import mybir

F32 = mybir.dt.float32
F32R = mybir.dt.float32r
BF16 = mybir.dt.bfloat16
ALU = mybir.AluOpType
ACT = mybir.ActivationFunctionType
AX = mybir.AxisListType

P = 128
D = 128
B, S = 4, 512
NT = S // P
G, HG, DH = 4, 4, 8
CONTEXT = 64
QB = 32
NQ = S // QB
WIN = CONTEXT + QB
PAD = CONTEXT
SCALE = DH ** -0.5
EPS = 1e-5

PAR, DEPTH = 8, 7
INNER = 2 ** DEPTH - 1
NODES = 2 ** (DEPTH + 1) - 1
BIG = 2.0 ** 80

RUNS = (3, 2, 1)
MASK_ROW = sum(RUNS) * DH
SHIFT_ROW = MASK_ROW + QB
SCORE_ROWS = 96
PHASES = 3
VW = G * DH
PV_ROWS = 2 * VW
QUAD = 4
NQUAD = NQ // QUAD

LN1_T, MODULATION, LN2_T, ROWS = 0, 1, 3, 5
MAX_T = ROWS + NQ
COLS = MAX_T + 1


def col_step(b):
    return COLS + b + max(0, (b - 1) // QUAD - 1)


def out_step(t):
    return COLS + min((t + 2) * QUAD + 1, NQ) + t


STEPS = out_step(NT - 1) + 1
N_SPLIT = 3
assert STEPS % 2 == 0


def projection_steps(a):
    return (2, 3, 4) if isinstance(a, int) and a == 0 else (1, 2, 4)


def split_steps(a):
    return [*projection_steps(a)[:2], MAX_T]


def reads(a, bank, step):
    return sum(n % 2 == bank and n not in split_steps(a) for n in range(step))


assert reads(0, 0, STEPS) == reads(1, 0, STEPS) and reads(0, 1, STEPS) == reads(1, 1, STEPS)


NP = 3
LAST_TURN = 6
FIRST_TURN = 2
ROW_TURNS = range(3, 6)
GATES = 6
LN1_STEPS = 2 * NT + 1
TILE_GROUPS = ((0,), (1,), (2, 3))
assert FIRST_TURN < ROW_TURNS[0]
assert QUAD * QB == P and NQUAD == NT and LAST_TURN == PAR - 2


def ln2_steps_before(group):
    return sum(2 * len(tiles) + 1 for tiles in TILE_GROUPS[:group])


def rows_of_turn(s):
    n, s = len(ROW_TURNS), s - ROW_TURNS[0]
    return list(range(NQ * s // n, NQ * (s + 1) // n)) if 0 <= s < n else []


def block_program(nc, x, wq, bq, wk, bk, wv, bv, wo, bo, w_in, b_in, w_out, c_t, wmod,
                  q_const, k_const, tree_in, ident_in, out):
    with ExitStack() as ctx:
        def sb(name, shape, dt=F32):
            return ctx.enter_context(nc.sbuf_tensor(name, shape, dt))

        def psum(name, shape):
            return ctx.enter_context(nc.psum_tensor(name, shape, F32))

        def sem(name):
            return ctx.enter_context(nc.semaphore(name))

        wq_sb, wk_sb, wv_sb = sb("wq_sb", [P, D]), sb("wk_sb", [P, P]), sb("wv_sb", [P, G * DH])
        wo_sb = sb("wo_sb", [P, D])
        bq_sb, bk_sb = sb("bq_sb", [P, 1]), sb("bk_sb", [P, 1])
        bv_sb, bo_sb = sb("bv_sb", [WIN, G * DH]), sb("bo_sb", [P, D])
        w_in_sb = sb("w_in_sb", [P, 2 * PAR, P])
        w_out_sb = sb("w_out_sb", [P, 2 * PAR, D])
        b_in_sb = sb("b_in_sb", [P, 2 * PAR])
        c_sb, wmod_sb = sb("c_sb", [P, B]), sb("wmod_sb", [P, 6 * D])
        w_in_hi, w_out_hi = (sb(f"{n}_hi", [P, 2 * PAR, P], F32R) for n in ("w_in", "w_out"))
        w_in_lo, w_out_lo = (sb(f"{n}_lo", [P, 2 * PAR, P], F32R) for n in ("w_in", "w_out"))
        tree = sb("tree", [P, 2, P], BF16)
        ident = sb("ident", [P, P])
        silu_c = sb("silu_c", [P, B])
        mod = sb("mod", [P, 5, B])
        gate_sign, gate_size = sb("gate_sign", [P, B, D]), sb("gate_size", [P, B, D])
        ga = sb("ga", [P, B, D])
        gb_sign, gb_size = sb("gb_sign", [P, B]), sb("gb_size", [P, B])
        wo_ga, bo_ga = sb("wo_ga", [P, B, D]), sb("bo_ga", [P, B, D])
        x_sb = sb("x_sb", [P, NT, D])
        xb = sb("xb", [P, NT, D])
        stats = sb("stats", [P, 2, NT, 6])
        moments = sb("moments", [P, 2, NT, 2])
        var_eps = sb("var_eps", [P, 2, NT])
        rstd = sb("rstd", [P, 2, NT])
        minus_half = sb("minus_half", [P, NT])
        xn = sb("xn", [P, 2, NT, D])
        h1 = sb("h1", [P, PAD + S])
        q_first, q_second, q_third = (sb(f"q_{n}", [P, S], BF16) for n in ("first", "second", "third"))
        q_rest = sb("q_rest", [P, S])
        k_first, k_second, k_third = (sb(f"k_{n}", [P, S], BF16) for n in ("first", "second", "third"))
        k_rest = sb("k_rest", [P, S])
        q_part = sb("q_part", [3 * VW, NQ, HG, QB], BF16)
        q_stack = sb("q_stack", [SCORE_ROWS, G, NQ, HG * QB], BF16)
        k_stack = sb("k_stack", [SCORE_ROWS, PHASES, G, PAD + S], BF16)
        v_win = sb("v_win", [WIN, NQ, G * (2 * VW + DH)])
        neg_max = sb("neg_max", [P, P])
        max_part = sb("max_part", [2 * G * NQ, P], BF16)
        probs = sb("probs", [WIN, NP, G * P])
        pv = sb("pv", [P, S])
        den = sb("den", [P, S])
        inv_den = sb("inv_den", [P, S])
        attn = sb("attn", [P, S])
        x1 = sb("x1", [P, NT, D])
        h2 = sb("h2", [P, S])
        h2_hi, h2_lo = sb("h2_hi", [P, S], F32R), sb("h2_lo", [P, S], F32R)
        x1_kept = sb("x1_kept", [P, NT, D])
        decided = sb("decided", [P, 2, S], BF16)
        acts = sb("acts", [P, 2, 2, S])
        acts_hi, acts_lo = sb("acts_hi", [P, 2, 2, S], F32R), sb("acts_lo", [P, 2, 2, S], F32R)
        y_t = sb("y_t", [P, S])
        y = sb("y", [P, NT, D])

        turn_bank = [psum(f"turn_bank{i}", [P, 512]) for i in range(2)]
        pv_bank = psum("pv_bank", [P, 512])
        inner_bank = [psum(f"inner_bank{i}", [P, 512]) for i in range(2)]
        leaf_bank = [psum(f"leaf_bank{i}", [P, 512]) for i in range(2)]
        sum_bank = psum("sum_bank", [P, 512])
        pv_banks = (pv_bank, inner_bank[1])

        small_loaded, mask_rows_loaded = sem("small_loaded"), sem("mask_rows_loaded")
        attn_w_loaded, mlp_w_loaded = sem("attn_w_loaded"), sem("mlp_w_loaded")
        padding_filled = sem("padding_filled")
        minus_half_filled = sem("minus_half_filled")
        silu_c_ready, output_gate_ready = sem("silu_c_ready"), sem("output_gate_ready")
        gb_steps, gate_steps = sem("gb_steps"), sem("gate_steps")
        first_x_loaded, x_loaded, xb_ready = sem("first_x_loaded"), sem("x_loaded"), sem("xb_ready")
        ln1_steps, rstd1_ready, xn1_ready = sem("ln1_steps"), sem("rstd1_ready"), sem("xn1_ready")
        ln2_steps, rstd2_ready, xn2_ready = sem("ln2_steps"), sem("rstd2_ready"), sem("xn2_ready")
        bank_filled = sem("bank_filled")
        bank_read = [sem(f"bank_read{i}") for i in range(2)]
        first_ready, rest_ready = sem("first_ready"), sem("rest_ready")
        second_ready, third_ready = sem("second_ready"), sem("third_ready")
        first_placed, later_placed = sem("first_placed"), sem("later_placed")
        q_stacked, k_stacked, phases_ready = sem("q_stacked"), sem("k_stacked"), sem("phases_ready")
        shift_loaded = sem("shift_loaded")
        v_filled = sem("v_filled")
        pv_done, den_ready, pv_ready = sem("pv_done"), sem("den_ready"), sem("pv_ready")
        inv_ready, attn_ready = sem("inv_ready"), sem("attn_ready")
        h2_hi_ready, h2_lo_ready, w_hi_ready = sem("h2_hi_ready"), sem("h2_lo_ready"), sem("w_hi_ready")
        w_split, acts_hi_ready, acts_lo_ready = sem("w_split"), sem("acts_hi_ready"), sem("acts_lo_ready")
        x1_kept_ready = sem("x1_kept_ready")
        logits_done, decided_ready = sem("logits_done"), sem("decided_ready")
        masked, acts_ready, summed = sem("masked"), sem("acts_ready"), sem("summed")
        y_t_ready, y_turned = sem("y_t_ready"), sem("y_turned")
        y_ready, y_stored = sem("y_ready"), sem("y_stored")

        STACK_DMAS = 16 * len(RUNS)
        N_SMALL, N_MASK_ROWS, N_ATTN_W, N_MLP_W = 16 * 3, 16 * 2, 16 * 8, 16 * 4

        def wait(eng, s, per, n, k):
            k = max(k, 0)
            if isinstance(n, int) and n * per + k == 0:
                return
            eng.wait_ge(s, n * per + k)

        def wait_read(eng, a, step):
            if step in split_steps(a):
                wait(eng, rest_ready, N_SPLIT, a, split_steps(a).index(step) + 1)
            else:
                wait(eng, bank_read[step % 2], reads(a, step % 2, STEPS), a, reads(a, step % 2, step + 1))

        def wait_free(eng, a, step):
            if step >= 2:
                wait_read(eng, a, step - 2)
            else:
                wait(eng, bank_read[step % 2], reads(a, step % 2, STEPS), a, 0)

        def wait_filled(eng, a, step):
            wait(eng, bank_filled, STEPS, a, step + 1)

        def ln2_at(a):
            return (B, LN1_T) if isinstance(a, int) and a == B - 1 else (a + 1, LN2_T)

        def col(n):
            return bass.ds(n, 1) if not isinstance(n, int) else slice(n, n + 1)

        x_tiles = x.rearrange("b (t p) d -> b p t d", p=P)
        out_tiles = out.rearrange("b (t p) d -> b p t d", p=P)

        def by_head(ap, rows, h, blocks):
            return ap[rows, :].rearrange("p (b h q) -> p b h q", h=HG, q=QB)[:, 0:blocks, h, :]

        v_groups = v_win[:, :, :].rearrange("p b (g c) -> p b g c", g=G)

        block = ctx.enter_context(nc.Block())

        @block.sync
        def _(sp):
            sp.dma_start(c_sb[:, :], c_t).then_inc(small_loaded, 16)
            sp.dma_start(wmod_sb[:, :], wmod).then_inc(small_loaded, 16)
            sp.dma_start(ident[:, :], ident_in).then_inc(small_loaded, 16)
            sp.dma_start(wq_sb[:, :], wq).then_inc(attn_w_loaded, 16)
            sp.dma_start(bq_sb[:, :], bq).then_inc(attn_w_loaded, 16)
            sp.dma_start(wk_sb[:, :], wk).then_inc(attn_w_loaded, 16)
            sp.dma_start(bk_sb[:, :], bk).then_inc(attn_w_loaded, 16)
            sp.dma_start(wv_sb[:, :], wv).then_inc(attn_w_loaded, 16)
            sp.dma_start(bv_sb[:, :], bv).then_inc(attn_w_loaded, 16)
            sp.dma_start(wo_sb[:, :], wo).then_inc(attn_w_loaded, 16)
            sp.dma_start(bo_sb[:, :], bo).then_inc(attn_w_loaded, 16)
            sp.dma_start(tree[:, :, :], tree_in.bitcast(BF16)).then_inc(mlp_w_loaded, 16)

            def stack_q_and_k(a, before):
                if before is not None:
                    wait_filled(sp, before, col_step(NQ - 1))
                parts = {1: (k_third, third_ready), 2: (k_second, second_ready), 3: (k_first, first_ready)}

                def rows_of(run):
                    row = MASK_ROW - sum(r for r in RUNS if r <= run) * DH
                    return slice(row, row + run * DH)

                def stack_q(run):
                    if run == 1:
                        wait(sp, first_placed, HG, a, HG)
                    else:
                        wait(sp, later_placed, 2 * HG, a, (run - 1) * HG)
                    sp.dma_start(q_stack[rows_of(run), :, :, :].rearrange("p g b c -> p g (b c)"),
                                 q_part[0:run * VW, :, :, :].rearrange("p b h q -> p (b h q)"))\
                        .then_inc(q_stacked, 16)

                def stack_k(run):
                    part, ready = parts[run]
                    wait(sp, ready, N_SPLIT if run == 3 else 2, a, 2)
                    sp.dma_start(k_stack[rows_of(run), 0, :, PAD:], part[0:run * VW, :])\
                        .then_inc(k_stacked, 16)

                for run in (3, 2, 1):
                    stack_k(run)
                for run in (1, 2, 3):
                    stack_q(run)

            def stack_max(a):
                wait(sp, first_ready, N_SPLIT, a, N_SPLIT)
                wait(sp, rest_ready, N_SPLIT, a, N_SPLIT)
                sp.dma_start(q_stack[SHIFT_ROW:SHIFT_ROW + 2, :, :, :].rearrange("p g b c -> p (g b) c"),
                             max_part[:, :]).then_inc(shift_loaded, 16)

            def load_x(n, a):
                wait(sp, xn1_ready, NT, a, NT)
                wait(sp, xb_ready, 1, a, 1)
                sp.dma_start(x_sb[:, :, :], x_tiles[n]).then_inc(x_loaded, 16)

            def store(f):
                wait(sp, y_ready, 1, f, 1)
                sp.dma_start(out_tiles[f], y[:, :, :]).then_inc(y_stored, 16)

            sp.wait_ge(mask_rows_loaded, N_MASK_ROWS)
            stack_q_and_k(0, None)
            stack_max(0)
            load_x(1, 0)
            stack_q_and_k(1, 0)
            load_x(2, 1)
            with sp.Fori(0, B - 3) as i:
                stack_max(i + 1)
                stack_q_and_k(i + 2, i + 1)
                store(i)
                load_x(i + 3, i + 2)
                wait(sp, y_stored, 16, i, 16)
            stack_max(B - 2)
            stack_q_and_k(B - 1, B - 2)
            for f in range(B - 3, B):
                store(f)
                sp.wait_ge(y_stored, 16 * (f + 1))
                if f == B - 3:
                    stack_max(B - 1)

        @block.gpsimd
        def _(pool):
            def inverse_deviations(a):
                wait(pool, ln1_steps, LN1_STEPS, a, LN1_STEPS)
                pool.tensor_tensor(rstd[:, 0, :], var_eps[:, 0, :], minus_half[:, :], ALU.pow)\
                    .then_inc(rstd1_ready, 1)

            def inverse_deviations_2(a, group):
                tiles = TILE_GROUPS[group]
                own = slice(tiles[0], tiles[-1] + 1)
                wait(pool, ln2_steps, ln2_steps_before(len(TILE_GROUPS)), a, ln2_steps_before(group + 1))
                pool.tensor_tensor(rstd[:, 1, own], var_eps[:, 1, own], minus_half[:, own],
                                   ALU.pow).then_inc(rstd2_ready, 1)

            def acts_low_parts(f, trees, halves=(0, 1)):
                for t in trees:
                    for n in halves:
                        wait(pool, acts_ready, 2 * PAR, f, 2 * t + n + 1)
                        pool.tensor_tensor(acts_lo[:, t % 2, n, :], acts[:, t % 2, n, :],
                                           acts_hi[:, t % 2, n, :].bitcast(F32), ALU.subtract)\
                            .then_inc(acts_lo_ready, 1)

            pool.memset(minus_half[:, :], -0.5).then_inc(minus_half_filled, 1)
            pool.wait_ge(minus_half_filled, 1)
            inverse_deviations(0)
            inverse_deviations(1)
            for group in range(len(TILE_GROUPS)):
                inverse_deviations_2(0, group)
            acts_low_parts(0, range(LAST_TURN))

            def iteration(i, a, after):
                if after is not None:
                    inverse_deviations(after)
                inverse_deviations_2(a, 0)
                inverse_deviations_2(a, 1)
                acts_low_parts(i, [LAST_TURN], [0])
                inverse_deviations_2(a, 2)
                acts_low_parts(i, [LAST_TURN], [1])
                acts_low_parts(i, [LAST_TURN + 1])
                acts_low_parts(a, range(LAST_TURN))

            with pool.Fori(0, B - 2) as i:
                iteration(i, i + 1, i + 2)
            iteration(B - 2, B - 1, None)
            acts_low_parts(B - 1, [LAST_TURN])

        @block.scalar
        def _(act):
            act.dma_start(x_sb[:, :, :], x_tiles[0]).then_inc(first_x_loaded, 16)
            act.wait_ge(small_loaded, N_SMALL)
            nc.scalar.activation(silu_c[:, :], c_sb[:, :], ACT.Silu).then_inc(silu_c_ready, 1)
            act.wait_ge(attn_w_loaded, N_ATTN_W)
            act.dma_start(q_stack[MASK_ROW:, :, :, :].rearrange("p g b c -> p g (b c)"),
                          q_const.bitcast(BF16).rearrange("p (g c) -> p g c", g=1)
                          .to_broadcast([SCORE_ROWS - MASK_ROW, G, HG * S]))\
                .then_inc(mask_rows_loaded, 16)
            act.dma_start(k_stack[MASK_ROW:, :, :, :].rearrange("p f g c -> p (f g) c"),
                          k_const.bitcast(BF16))\
                .then_inc(mask_rows_loaded, 16)
            act.dma_start(w_in_sb[:, :, :], w_in).then_inc(mlp_w_loaded, 16)
            act.dma_start(w_out_sb[:, :, :], w_out).then_inc(mlp_w_loaded, 16)
            act.dma_start(b_in_sb[:, :], b_in).then_inc(mlp_w_loaded, 16)

            def first_h(a):
                if isinstance(a, int) and a == 0:
                    wait_read(act, 0, MODULATION)
                wait_filled(act, a, LN1_T)
                nc.scalar.activation(h1[:, PAD:], turn_bank[LN1_T % 2][:, :], ACT.Identity,
                                     bias=mod[:, 0, col(a)], scale=mod[:, 1, col(a)])\
                    .then_inc(bank_read[LN1_T % 2], 1)

            def first_parts(a):
                wait(act, q_stacked, STACK_DMAS, a, 0)
                wait(act, k_stacked, STACK_DMAS, a, 0)
                step_q, step_k, _ = projection_steps(a)
                wait_filled(act, a, step_q)
                nc.scalar.activation(q_first[:, :], turn_bank[step_q % 2][:, :], ACT.Identity,
                                     bias=bq_sb[:, :]).then_inc(first_ready, 1)
                wait_filled(act, a, step_k)
                nc.scalar.activation(k_first[:, :], turn_bank[step_k % 2][:, :], ACT.Identity,
                                     bias=bk_sb[:, :]).then_inc(first_ready, 1)

            def place_first(a):
                wait(act, first_ready, N_SPLIT, a, 1)
                for h in range(HG):
                    nc.scalar.activation(q_part[0:VW, :, h, :],
                                         q_first[h * VW:(h + 1) * VW, :].rearrange("p (b q) -> p b q", q=QB),
                                         ACT.Identity).then_inc(first_placed, 1)

            def round_max(a):
                wait_filled(act, a, MAX_T)
                wait(act, shift_loaded, 16, a, 0)
                nc.scalar.activation(max_part[0:G * NQ, :], turn_bank[MAX_T % 2][0:G * NQ, 0:P],
                                     ACT.Identity).then_inc(first_ready, 1)

            def exps(a):
                for b in range(NQ):
                    step = col_step(b)
                    if b >= NP:
                        wait(act, pv_done, NQ, a, b - NP + 1)
                    wait_filled(act, a, step)
                    nc.scalar.activation(probs[:, b % NP, :], turn_bank[step % 2][0:WIN, :], ACT.Exp,
                                         scale=SCALE).then_inc(bank_read[step % 2], 1)
                    if b % QUAD == 0 and b > 0:
                        sums(a, b // QUAD - 1)
                sums(a, NQUAD - 1)

            def sums(a, n):
                wait(act, pv_done, NQ, a, (n + 1) * QUAD)
                for h in range(HG):
                    ins = nc.scalar.activation(
                        den[h * VW:(h + 1) * VW, n * P:(n + 1) * P].rearrange("p (b q) -> p b q", q=QB),
                        by_head(pv_banks[n % 2], slice(VW, PV_ROWS), h, QUAD), ACT.Identity)
                ins.then_inc(den_ready, 1)

            def second_h(a):
                at, step = ln2_at(a)
                wait_filled(act, at, step)
                wait(act, logits_done, 2 * PAR, a, 0)
                for h, done in ((h2_hi, h2_hi_ready), (h2, bank_read[step % 2])):
                    nc.scalar.activation(h[:, :], turn_bank[step % 2][:, :], ACT.Identity,
                                         bias=mod[:, 2, col(a)], scale=mod[:, 3, col(a)]).then_inc(done, 1)

            def silus(t, f, halves=(0, 1)):
                for n in halves:
                    bank = (inner_bank, leaf_bank)[n]
                    wait(act, masked, 2 * PAR, f, 2 * t + n + 1)
                    if t >= 2:
                        wait(act, summed, PAR, f, t - 1)
                    for act_of, done in ((acts_hi, acts_hi_ready), (acts, acts_ready)):
                        nc.scalar.activation(act_of[:, t % 2, n, :], bank[t % 2][:, :], ACT.Silu,
                                             bias=b_in_sb[:, 2 * t + n:2 * t + n + 1]).then_inc(done, 1)

            def iteration(i, a, after):
                for t in range(FIRST_TURN, LAST_TURN):
                    silus(t, i)
                round_max(a)
                exps(a)
                silus(PAR - 2, i)
                if after is not None:
                    first_h(after)
                silus(PAR - 1, i, [0])
                if after is not None:
                    first_parts(after)
                silus(PAR - 1, i, [1])
                second_h(a)
                if after is not None:
                    place_first(after)
                silus(0, a)
                silus(1, a)

            first_h(0)
            first_parts(0)
            place_first(0)
            round_max(0)
            exps(0)
            first_h(1)
            first_parts(1)
            second_h(0)
            place_first(1)
            act.wait_ge(mlp_w_loaded, N_MLP_W)
            silus(0, 0)
            silus(1, 0)
            with act.Fori(0, B - 2) as i:
                iteration(i, i + 1, i + 2)
            iteration(B - 2, B - 1, None)
            for t in range(FIRST_TURN, PAR):
                silus(t, B - 1)

        @block.vector
        def _(dve):
            dve.memset(h1[:, 0:PAD], 0.0)
            dve.memset(neg_max[:, G * NQ:], 0.0)
            dve.memset(k_stack[0:MASK_ROW, :, :, 0:PAD], 0.0).then_inc(padding_filled, 1)

            def fill_v(half):
                own = slice(half * NQ // 2, (half + 1) * NQ // 2)
                dve.memset(v_win[:, own, :], 0.0).then_inc(v_filled, 1)
                dve.wait_ge(v_filled, 2 * half + 1)
                dve.memset(v_groups[:, own, :, VW:VW + DH], 1.0).then_inc(v_filled, 1)

            def token_stats(a):
                if isinstance(a, int) and a == 0:
                    dve.wait_ge(first_x_loaded, 16)
                else:
                    wait(dve, x_loaded, 16, a - 1, 16)
                for t in range(NT):
                    dve.bn_stats(stats[:, 0, t, :], x_sb[:, t, :]).then_inc(ln1_steps, 1)
                wait(dve, ln1_steps, LN1_STEPS, a, NT)

            def token_moments(a):
                for t in range(NT):
                    dve.bn_aggr(moments[:, 0, t, :], stats[:, 0, t, :]).then_inc(ln1_steps, 1)
                wait(dve, ln1_steps, LN1_STEPS, a, 2 * NT)
                dve.tensor_scalar(var_eps[:, 0, :], moments[:, 0, :, 1], EPS, None, ALU.add)\
                    .then_inc(ln1_steps, 1)

            def normalized(n, t, src):
                return dve.tensor_scalar(xn[:, n, t, :], src[:, t, :], moments[:, n, t, 0:1],
                                         rstd[:, n, t:t + 1], ALU.subtract, ALU.mult)

            def normalize(a, t):
                if t == 0:
                    wait(dve, rstd1_ready, 1, a, 1)
                normalized(0, t, x_sb).then_inc(xn1_ready, 1)

            def attention_bias(a):
                if not (isinstance(a, int) and a == 0):
                    wait_read(dve, a - 1, out_step(NT - 1))
                dve.tensor_tensor(xb[:, :, :], x_sb[:, :, :],
                                  bo_ga[:, col(a), :].to_broadcast([P, NT, D]), ALU.add)\
                    .then_inc(xb_ready, 1)

            def sides(a):
                step_q, step_k, _ = projection_steps(a)
                return ((turn_bank[step_q % 2], bq_sb, q_first, q_rest, q_second, q_third),
                        (turn_bank[step_k % 2], bk_sb, k_first, k_rest, k_second, k_third))

            def rest(a, n):
                if n == 0:
                    wait(dve, q_stacked, STACK_DMAS, a, 0)
                    wait(dve, k_stacked, STACK_DMAS, a, 0)
                bank, bias, first, rest, _, _ = sides(a)[n]
                wait(dve, first_ready, N_SPLIT, a, n + 1)
                dve.scalar_tensor_tensor(out=rest[:, :], in0=bank[:, :], scalar=bias[:, :], in1=first[:, :],
                                         op0=ALU.add, op1=ALU.subtract).then_inc(rest_ready, 1)

            def later_parts(a):
                for n, (_, _, _, rest, second, _) in enumerate(sides(a)):
                    wait(dve, rest_ready, N_SPLIT, a, n + 1)
                    dve.tensor_copy(second[:, :], rest[:, :]).then_inc(second_ready, 1)
                for n, (_, _, _, rest, second, third) in enumerate(sides(a)):
                    wait(dve, second_ready, 2, a, n + 1)
                    dve.tensor_tensor(third[:, :], rest[:, :], second[:, :], ALU.subtract)\
                        .then_inc(third_ready, 1)

            def place_heads(a, n, part):
                if n == 2:
                    wait(dve, third_ready, 2, a, 1)
                for h in range(HG):
                    dve.tensor_copy(q_part[n * VW:(n + 1) * VW, :, h, :],
                                    part[h * VW:(h + 1) * VW, :].rearrange("p (b q) -> p b q", q=QB))\
                        .then_inc(later_placed, 1)

            def phases(a):
                wait(dve, k_stacked, STACK_DMAS, a, STACK_DMAS)
                for n in range(1, PHASES):
                    dve.tensor_copy(k_stack[0:MASK_ROW, n, :, PAD:], k_stack[0:MASK_ROW, 0, :, PAD:])\
                        .then_inc(phases_ready, 1)

            def values(a):
                step = projection_steps(a)[2]
                wait_filled(dve, a, step)
                dve.tensor_tensor(
                    v_groups[:, :, :, 0:DH],
                    turn_bank[step % 2][0:WIN, :].rearrange("p (b g d) -> p b g d", g=G, d=DH),
                    bv_sb[:, None, :].rearrange("p o (g d) -> p o g d", g=G)
                    .to_broadcast([WIN, NQ, G, DH]), ALU.add).then_inc(bank_read[step % 2], 1)

            def row_max(a, b):
                wait_filled(dve, a, ROWS + b)
                dve.tensor_reduce(neg_max[:, b:G * NQ:NQ],
                                  turn_bank[(ROWS + b) % 2][:, 0:G * WIN].rearrange("p (g k) -> p g k", g=G),
                                  AX.X, ALU.max, negate=True).then_inc(bank_read[(ROWS + b) % 2], 1)

            def max_low_part(a):
                wait_filled(dve, a, MAX_T)
                wait(dve, first_ready, N_SPLIT, a, N_SPLIT)
                wait(dve, shift_loaded, 16, a, 0)
                dve.tensor_tensor(max_part[G * NQ:, :], turn_bank[MAX_T % 2][0:G * NQ, 0:P],
                                  max_part[0:G * NQ, :], ALU.subtract).then_inc(rest_ready, 1)

            def products(a, n):
                wait(dve, pv_done, NQ, a, (n + 1) * QUAD)
                for h in range(HG):
                    ins = dve.tensor_copy(
                        pv[h * VW:(h + 1) * VW, n * P:(n + 1) * P].rearrange("p (b q) -> p b q", q=QB),
                        by_head(pv_banks[n % 2], slice(0, VW), h, QUAD))
                ins.then_inc(pv_ready, 1)

            def divide(a, n):
                own = slice(n * P, (n + 1) * P)
                wait(dve, den_ready, NQUAD, a, n + 1)
                dve.reciprocal(inv_den[:, own], den[:, own]).then_inc(inv_ready, 1)
                wait(dve, pv_ready, NQUAD, a, n + 1)
                wait(dve, inv_ready, NQUAD, a, n + 1)
                dve.tensor_tensor(attn[:, own], pv[:, own], inv_den[:, own], ALU.mult).then_inc(attn_ready, 1)

            def first_residual(a, group):
                per = ln2_steps_before(len(TILE_GROUPS))
                tiles = TILE_GROUPS[group]
                if group == 0:
                    wait(dve, xb_ready, 1, a, 1)
                    wait(dve, x1_kept_ready, 1, a, 0)
                for t in tiles:
                    step = out_step(t)
                    wait_filled(dve, a, step)
                    dve.tensor_tensor(x1[:, t, :], turn_bank[step % 2][:, 0:D], xb[:, t, :], ALU.add)\
                        .then_inc(bank_read[step % 2], 1)
                for t in tiles:
                    wait_read(dve, a, out_step(t))
                    dve.bn_stats(stats[:, 1, t, :], x1[:, t, :]).then_inc(ln2_steps, 1)
                wait(dve, ln2_steps, per, a, ln2_steps_before(group) + len(tiles))

            def tile_moments(a, group):
                per = ln2_steps_before(len(TILE_GROUPS))
                tiles = TILE_GROUPS[group]
                for t in tiles:
                    dve.bn_aggr(moments[:, 1, t, :], stats[:, 1, t, :]).then_inc(ln2_steps, 1)
                wait(dve, ln2_steps, per, a, ln2_steps_before(group) + 2 * len(tiles))
                own = slice(tiles[0], tiles[-1] + 1)
                dve.tensor_scalar(var_eps[:, 1, own], moments[:, 1, own, 1], EPS, None, ALU.add)\
                    .then_inc(ln2_steps, 1)

            def normalize_2(a, group):
                wait(dve, rstd2_ready, len(TILE_GROUPS), a, group + 1)
                for t in TILE_GROUPS[group]:
                    ins = normalized(1, t, x1)
                ins.then_inc(xn2_ready, 1)

            def outputs(i, a, after):
                if after is not None:
                    token_stats(after)
                products(a, 0)
                divide(a, 0)
                if after is not None:
                    token_moments(after)
                first_residual(a, 0)
                if after is not None:
                    normalize(after, 0)
                    normalize(after, 1)
                tile_moments(a, 0)
                products(a, 1)
                divide(a, 1)
                first_residual(a, 1)
                normalize_2(a, 0)
                tile_moments(a, 1)
                products(a, 2)
                divide(a, 2)
                if after is not None:
                    normalize(after, 2)
                    normalize(after, 3)
                products(a, 3)
                divide(a, 3)
                if i is not None:
                    decisions(PAR - 1, i)
                first_residual(a, 2)
                normalize_2(a, 1)
                tile_moments(a, 2)

            def h2_low_part(a):
                wait_read(dve, *ln2_at(a))
                dve.tensor_tensor(h2_lo[:, :], h2[:, :], h2_hi[:, :].bitcast(F32), ALU.subtract)\
                    .then_inc(h2_lo_ready, 1)

            def keep_x1(a):
                dve.tensor_copy(x1_kept[:, :, :], x1[:, :, :]).then_inc(x1_kept_ready, 1)

            def decisions(t, f):
                wait(dve, logits_done, 2 * PAR, f, 2 * t + 1)
                if t >= 2:
                    wait(dve, masked, 2 * PAR, f, 2 * t - 2)
                dve.tensor_scalar(decided[:, t % 2, :], inner_bank[t % 2][:, :],
                                  b_in_sb[:, 2 * t:2 * t + 1], 0.0, ALU.add, ALU.is_gt)\
                    .then_inc(decided_ready, 1)

            def last_acts_low_part():
                dve.wait_ge(acts_lo_ready, 2 * PAR * B - 2)
                for n in range(2):
                    dve.wait_ge(acts_ready, 2 * PAR * B - 1 + n)
                    t = PAR - 1
                    dve.tensor_tensor(acts_lo[:, t % 2, n, :], acts[:, t % 2, n, :],
                                      acts_hi[:, t % 2, n, :].bitcast(F32), ALU.subtract)\
                        .then_inc(acts_lo_ready, 1)

            def scale_sum(f):
                wait(dve, summed, PAR, f, PAR)
                dve.tensor_scalar(y_t[:, :], sum_bank[:, :], mod[:, 4, col(f)], None, ALU.mult)\
                    .then_inc(y_t_ready, 1)

            def second_residual(f):
                wait(dve, y_turned, 1, f, 1)
                wait(dve, x1_kept_ready, 1, f, 1)
                if isinstance(f, int):
                    wait(dve, y_stored, 16, f, 0)
                dve.tensor_tensor(y[:, :, :], sum_bank[:, :].rearrange("p (t d) -> p t d", d=D),
                                  x1_kept[:, :, :], ALU.add).then_inc(y_ready, 1)

            def signed_size(sign, size, gate, src, done, n):
                dve.tensor_scalar(sign, src, 0.0, 2.0, ALU.is_ge, ALU.mult).then_inc(done, 1)
                dve.wait_ge(done, n + 1)
                dve.scalar_tensor_tensor(out=size, in0=sign, scalar=-1.0, in1=src,
                                         op0=ALU.add, op1=ALU.mult).then_inc(done, 1)
                dve.wait_ge(done, n + 2)
                dve.tensor_scalar(size, size, 0.25, None, ALU.max).then_inc(done, 1)
                dve.wait_ge(done, n + 3)
                dve.scalar_tensor_tensor(out=gate, in0=sign, scalar=-1.0, in1=size,
                                         op0=ALU.add, op1=ALU.mult).then_inc(done, 1)

            def gates():
                wait_filled(dve, 0, MODULATION)
                m = turn_bank[MODULATION % 2][:, 0:5 * B].rearrange("p (j b) -> p j b", b=B)
                dve.tensor_copy(mod[:, 0:5:2, :], m[:, 0:5:2, :])
                dve.tensor_scalar(mod[:, 1:4:2, :], m[:, 1:4:2, :], 1.0, None, ALU.add)\
                    .then_inc(bank_read[MODULATION % 2], 1)
                wait_read(dve, 0, MODULATION)
                signed_size(gb_sign[:, :], gb_size[:, :], mod[:, 4, :], mod[:, 4, :], gb_steps, 0)

            def gate_output():
                dve.wait_ge(output_gate_ready, 1)
                m = sum_bank[:, :].rearrange("p (b d) -> p b d", d=D)
                signed_size(gate_sign[:, :, :], gate_size[:, :, :], ga[:, :, :], m, gate_steps, 0)
                dve.wait_ge(gate_steps, 4)
                for src, dst in ((wo_sb, wo_ga), (bo_sb, bo_ga)):
                    dve.tensor_tensor(dst[:, :, :], src[:, None, :].to_broadcast([P, B, D]), ga[:, :, :],
                                      ALU.mult).then_inc(gate_steps, 1)

            def after_outputs(i, a, after):
                normalize_2(a, 2)
                if after is not None:
                    rest(after, 0)
                    rest(after, 1)
                    later_parts(after)
                h2_low_part(a)
                if after is not None:
                    values(after)
                    place_heads(after, 1, q_second)
                decisions(0, a)
                if after is not None:
                    place_heads(after, 2, q_third)
                if i is not None:
                    scale_sum(i)
                decisions(1, a)
                if i is not None:
                    second_residual(i)
                    wait(dve, y_ready, 1, i, 1)
                keep_x1(a)
                decisions(2, a)
                if after is not None:
                    phases(after)
                    attention_bias(after)

            def iteration(i, a, after):
                for t in range(FIRST_TURN + 1, LAST_TURN + 1):
                    decisions(t, i)
                    for b in rows_of_turn(t):
                        row_max(a, b)
                    if t == ROW_TURNS[-1]:
                        max_low_part(a)
                outputs(i, a, after)
                after_outputs(i, a, after)

            fill_v(0)
            token_stats(0)
            token_moments(0)
            for t in range(NT):
                normalize(0, t)
            gates()
            fill_v(1)
            dve.wait_ge(attn_w_loaded, N_ATTN_W)
            rest(0, 0)
            rest(0, 1)
            later_parts(0)
            place_heads(0, 1, q_second)
            place_heads(0, 2, q_third)
            dve.wait_ge(v_filled, 4)
            values(0)
            phases(0)
            for b in range(NQ):
                row_max(0, b)
            max_low_part(0)
            gate_output()
            dve.wait_ge(gate_steps, GATES)
            attention_bias(0)
            dve.wait_ge(mlp_w_loaded, N_MLP_W)
            for w, hi, lo in ((w_in_sb, w_in_hi, w_in_lo), (w_out_sb, w_out_hi, w_out_lo)):
                dve.tensor_copy(hi[:, :, :], w[:, :, :]).then_inc(w_hi_ready, 1)
            for n, (w, hi, lo) in enumerate(((w_in_sb, w_in_hi, w_in_lo), (w_out_sb, w_out_hi, w_out_lo))):
                dve.wait_ge(w_hi_ready, n + 1)
                dve.tensor_tensor(lo[:, :, :], w[:, :, :], hi[:, :, :].bitcast(F32), ALU.subtract)\
                    .then_inc(w_split, 1)
            outputs(None, 0, 1)
            after_outputs(None, 0, 1)

            with dve.Fori(0, B - 2) as i:
                iteration(i, i + 1, i + 2)
            iteration(B - 2, B - 1, None)
            for t in range(FIRST_TURN + 1, PAR):
                decisions(t, B - 1)
            last_acts_low_part()
            scale_sum(B - 1)
            second_residual(B - 1)

        @block.tensor
        def _(pe):
            def modulation():
                pe.wait_ge(silu_c_ready, 1)
                for j, part in enumerate((0, 1, 3, 4, 5)):
                    ins = pe.matmul(turn_bank[MODULATION % 2][:, j * B:(j + 1) * B],
                                    wmod_sb[:, part * D:(part + 1) * D],
                                    silu_c[:, :], start=True, stop=True)
                ins.then_inc(bank_filled, 1)

            def output_gate():
                for b in range(B):
                    ins = pe.matmul(sum_bank[:, b * D:(b + 1) * D], silu_c[:, b:b + 1].to_broadcast([P, P]),
                                    wmod_sb[:, 2 * D:3 * D], start=True, stop=True)
                ins.then_inc(output_gate_ready, 1)

            def turn_xn(n, at, step):
                wait_free(pe, at, step)
                for t in range(NT):
                    ins = pe.transpose(turn_bank[step % 2][:, t * P:(t + 1) * P], xn[:, n, t, :], ident[:, :])
                ins.then_inc(bank_filled, 1)

            def turn_first(a):
                wait(pe, xn1_ready, NT, a, NT)
                turn_xn(0, a, LN1_T)

            def turn_second(a):
                wait(pe, xn2_ready, len(TILE_GROUPS), a, len(TILE_GROUPS))
                turn_xn(1, *ln2_at(a))

            def project_q_and_k(a):
                wait_read(pe, a, LN1_T)
                step_q, step_k, _ = projection_steps(a)
                wait_free(pe, a, step_q)
                pe.matmul(turn_bank[step_q % 2][:, :], wq_sb[:, :], h1[:, PAD:], start=True, stop=True)\
                    .then_inc(bank_filled, 1)
                wait_free(pe, a, step_k)
                pe.matmul(turn_bank[step_k % 2][:, :], wk_sb[:, :], h1[:, PAD:], start=True, stop=True)\
                    .then_inc(bank_filled, 1)

            def project_v(a):
                wait_read(pe, a, LN1_T)
                step = projection_steps(a)[2]
                wait_free(pe, a, step)
                for b in range(NQ):
                    ins = pe.matmul(turn_bank[step % 2][0:WIN, b * VW:(b + 1) * VW],
                                    h1[:, b * QB:b * QB + WIN], wv_sb[:, :], start=True, stop=True)
                ins.then_inc(bank_filled, 1)

            def q_block(g, b, rows):
                return q_stack[0:rows, g, b, :]

            def k_window(g, b, rows):
                return k_stack[0:rows, b % PHASES, g, b * QB:b * QB + WIN]

            def score_rows(a, b):
                if b == 0:
                    wait(pe, q_stacked, STACK_DMAS, a, STACK_DMAS)
                    wait(pe, k_stacked, STACK_DMAS, a, STACK_DMAS)
                    wait(pe, phases_ready, PHASES - 1, a, PHASES - 1)
                wait_free(pe, a, ROWS + b)
                for g in range(G):
                    ins = pe.matmul(turn_bank[(ROWS + b) % 2][:, g * WIN:(g + 1) * WIN],
                                    q_block(g, b, SHIFT_ROW), k_window(g, b, SHIFT_ROW),
                                    start=True, stop=True)
                ins.then_inc(bank_filled, 1)

            def whole(part, t, f):
                if f is not None:
                    part(t, 0, f)
                    part(t, 1, f)

            def turn_max(a):
                wait_read(pe, a, MAX_T - 2)
                wait_read(pe, a, MAX_T - 1)
                pe.transpose(turn_bank[MAX_T % 2][:, 0:P], neg_max[:, :], ident[:, :])\
                    .then_inc(bank_filled, 1)

            def score_cols(a, b):
                if b == 0:
                    wait(pe, shift_loaded, 16, a, 16)
                step = col_step(b)
                wait_free(pe, a, step)
                for g in range(G):
                    ins = pe.matmul(turn_bank[step % 2][0:WIN, g * P:(g + 1) * P],
                                    k_window(g, b, SCORE_ROWS), q_block(g, b, SCORE_ROWS),
                                    start=True, stop=True)
                ins.then_inc(bank_filled, 1)

            def times_v(a, b):
                step = col_step(b)
                wait_read(pe, a, step)
                n = b // QUAD
                if b == 0:
                    wait_read(pe, a, projection_steps(a)[2])
                    wait(pe, den_ready, NQUAD, a, 0)
                    wait(pe, pv_ready, NQUAD, a, 0)
                if n >= 2 and b % QUAD == 0:
                    wait(pe, den_ready, NQUAD, a, n - 1)
                    wait(pe, pv_ready, NQUAD, a, n - 1)
                for g in range(G):
                    ins = pe.matmul(pv_banks[n % 2][0:PV_ROWS, (b % QUAD) * P:(b % QUAD + 1) * P],
                                    v_win[:, b, g * PV_ROWS:(g + 1) * PV_ROWS],
                                    probs[:, b % NP, g * P:(g + 1) * P], start=(g == 0), stop=(g == G - 1))
                ins.then_inc(pv_done, 1)

            def attend(i, a):
                if i is not None:
                    sum_nodes(LAST_TURN - 1, 0, i)
                score_cols(a, 0)
                for b in range(1, NQ):
                    score_cols(a, b)
                    if b == 1:
                        whole(mask, LAST_TURN, i)
                    times_v(a, b - 1)
                    if b % QUAD == 0 and b > QUAD:
                        project_out(a, b // QUAD - 2)
                times_v(a, NQ - 1)
                project_out(a, NT - 2)

            def project_out(a, t):
                step = out_step(t)
                if isinstance(a, int) and a + t == 0:
                    pe.wait_ge(gate_steps, GATES)
                wait(pe, attn_ready, NQUAD, a, t + 1)
                wait_free(pe, a, step)
                pe.matmul(turn_bank[step % 2][:, 0:D], attn[:, t * P:(t + 1) * P], wo_ga[:, col(a), :],
                          start=True, stop=True).then_inc(bank_filled, 1)

            def logits(t, n, f):
                if t + n == 0:
                    wait(pe, h2_hi_ready, 1, f, 1)
                if t < 2:
                    wait(pe, acts_ready, 2 * PAR, f, 0)
                else:
                    wait(pe, acts_ready, 2 * PAR, f, 2 * (t - 2) + n + 1)
                into = (inner_bank, leaf_bank)[n][t % 2][:, :]
                for k, (w, h) in enumerate(((w_in_hi, h2_hi), (w_in_lo, h2_hi), (w_in_hi, h2_lo))):
                    if t + n == 0 and h is h2_lo:
                        wait(pe, h2_lo_ready, 1, f, 1)
                    ins = pe.matmul(into, w[:, 2 * t + n, :], h[:, :], start=(k == 0), stop=False,
                                    skip_group_check=True)
                ins.then_inc(logits_done, 1)

            def mask(t, n, f):
                if n == 0:
                    wait(pe, decided_ready, PAR, f, t + 1)
                pe.matmul((inner_bank, leaf_bank)[n][t % 2][:, :], tree[:, n, :], decided[:, t % 2, :],
                          start=False, stop=True, skip_group_check=True).then_inc(masked, 1)

            def sum_nodes(t, half, f):
                if t + half == 0:
                    wait(pe, x1_kept_ready, 1, f, 1)
                products = [(n, w, h) for n in range(2)
                            for w, h in ((w_out_hi, acts_hi), (w_out_lo, acts_hi))]
                products += [(n, w_out_hi, acts_lo) for n in range(2)]
                for k in ((0, 1, 2, 3), (4, 5))[half]:
                    n, w, h = products[k]
                    if w is w_out_hi:
                        wait(pe, acts_hi_ready if h is acts_hi else acts_lo_ready, 2 * PAR, f, 2 * t + n + 1)
                    ins = pe.matmul(sum_bank[:, :], w[:, 2 * t + n, :], h[:, t % 2, n, :],
                                    start=(t + k == 0), stop=(t == PAR - 1 and k == 5))
                if half == 1:
                    ins.then_inc(summed, 1)

            def turn_sum(f):
                wait(pe, y_t_ready, 1, f, 1)
                for t in range(NT):
                    ins = pe.transpose(sum_bank[:, t * P:(t + 1) * P], y_t[:, t * P:(t + 1) * P], ident[:, :])
                ins.then_inc(y_turned, 1)

            def tree_turn(s, f, a=None):
                rows = rows_of_turn(s) if a is not None else []
                for part, t in ((logits, s), (sum_nodes, s - 2), (mask, s)):
                    for n in range(2):
                        if 0 <= t < PAR and not (a is not None and part is mask and t == LAST_TURN):
                            part(t, n, f)
                        if rows:
                            score_rows(a, rows.pop(0))

            def after_attend(i, a, after):
                last = PAR - 1
                if i is not None:
                    sum_nodes(last - 2, 1, i)
                wait(pe, den_ready, NQUAD, a, NQUAD)
                wait(pe, pv_ready, NQUAD, a, NQUAD)
                whole(logits, last, i)
                project_out(a, NT - 1)
                whole(mask, last, i)
                if after is not None:
                    turn_first(after)
                if i is not None:
                    sum_nodes(last - 1, 0, i)
                if after is not None:
                    project_q_and_k(after)
                turn_second(a)
                if i is not None:
                    sum_nodes(last - 1, 1, i)
                if after is not None:
                    project_v(after)
                if i is None:
                    pe.wait_ge(w_split, 2)
                whole(logits, 0, a)
                whole(sum_nodes, last, i)
                whole(mask, 0, a)
                whole(logits, 1, a)
                if i is not None:
                    turn_sum(i)
                whole(mask, 1, a)

            def iteration(i, a, after):
                for s in range(FIRST_TURN, LAST_TURN + 1):
                    tree_turn(s, i, a)
                    if s == ROW_TURNS[-1]:
                        turn_max(a)
                attend(i, a)
                after_attend(i, a, after)

            pe.wait_ge(small_loaded, N_SMALL)
            turn_first(0)
            modulation()
            output_gate()
            pe.wait_ge(attn_w_loaded, N_ATTN_W)
            project_q_and_k(0)
            project_v(0)
            pe.wait_ge(mask_rows_loaded, N_MASK_ROWS)
            pe.wait_ge(padding_filled, 1)
            for b in range(NQ):
                score_rows(0, b)
            turn_max(0)
            attend(None, 0)
            after_attend(None, 0, 1)
            pe.wait_ge(mlp_w_loaded, N_MLP_W)

            with pe.Fori(0, B - 2) as i:
                iteration(i, i + 1, i + 2)
            iteration(B - 2, B - 1, None)
            for s in range(FIRST_TURN, PAR + 2):
                tree_turn(s, B - 1)
            turn_sum(B - 1)


def as_bf16(constants):
    import numpy as np
    return (constants.view(np.uint32) >> 16).astype(np.uint16)


def mask_rows():
    import numpy as np
    q = np.zeros((SCORE_ROWS - MASK_ROW, NQ * HG, QB), np.float32)
    k = np.zeros((SCORE_ROWS - MASK_ROW, PHASES, G, PAD + S), np.float32)
    for i in range(QB):
        q[i, :, i] = 1.0
        for phase in range(PHASES):
            place = (np.arange(PAD + S) - phase * QB) % WIN
            k[i, phase, :, (place <= i) | (place - CONTEXT > i)] = -BIG
    k[:QB, :, :, :PAD] = -BIG
    k[QB:QB + 2] = 1.0
    return as_bf16(q.reshape(-1, HG * S)), as_bf16(k.reshape(-1, PHASES * G, PAD + S))


def tree_matrices():
    import numpy as np
    m = np.zeros((P, 2 * P), np.float32)
    for node in range(NODES):
        at = node if node < INNER else P + node - INNER
        rights = 0
        below = node
        while below:
            above, right = (below - 1) // 2, below % 2 == 0
            m[above, at] = BIG if right else -BIG
            rights += right
            below = above
        m[P - 1, at] = -BIG * rights
    return as_bf16(m.reshape(P, 2, P))


def kernel(L0_attn_x, L0_attn_Wq, L0_attn_bq, L0_attn_Wk, L0_attn_bk, L0_attn_Wv, L0_attn_bv, L0_attn_Wo,
           L0_attn_bo, L0_ffn_W_in, L0_ffn_b_in, L0_ffn_W_out, L0_c, L0_wmod):
    import numpy as np
    import concourse.bacc as bacc
    from concourse.bass_utils import run_bass_kernel_spmd

    f = np.ascontiguousarray
    w_in = np.zeros((PAR, 2 * P, D), np.float32)
    w_out = np.zeros((PAR, 2 * P, D), np.float32)
    b_in = np.ones((PAR, 2 * P), np.float32)
    for dst, src in ((w_in, np.asarray(L0_ffn_W_in).reshape(PAR, NODES, D)),
                     (w_out, np.asarray(L0_ffn_W_out).T.reshape(PAR, NODES, D)),
                     (b_in, np.asarray(L0_ffn_b_in).reshape(PAR, NODES))):
        dst[:, :INNER] = src[:, :INNER]
        dst[:, P:] = src[:, INNER:]
    q_const, k_const = mask_rows()
    wq = np.asarray(L0_attn_Wq).reshape(D, G, HG, DH).transpose(0, 2, 3, 1).reshape(D, D)
    bq = np.asarray(L0_attn_bq).reshape(G, HG, DH).transpose(1, 2, 0).reshape(D, 1)
    wk = np.tile(np.asarray(L0_attn_Wk).reshape(D, G, DH).transpose(0, 2, 1).reshape(D, VW), (1, P // VW))
    bk = np.tile(np.asarray(L0_attn_bk).reshape(G, DH).T.reshape(VW, 1), (P // VW, 1))
    wo = np.asarray(L0_attn_Wo).reshape(G, HG, DH, D).transpose(1, 0, 2, 3).reshape(D, D)
    arrays = {
        "x": f(L0_attn_x), "wq": f(wq), "bq": f(bq),
        "wk": f(wk), "bk": f(bk),
        "wv": f(L0_attn_Wv), "bv": f(np.broadcast_to(np.asarray(L0_attn_bv), (WIN, G * DH))),
        "wo": f(wo), "bo": f(np.broadcast_to(np.asarray(L0_attn_bo), (P, D))),
        "w_in": f(w_in.reshape(2 * PAR, P, D).transpose(2, 0, 1)),
        "b_in": f(b_in.reshape(2 * PAR, P).T),
        "w_out": f(w_out.reshape(2 * PAR, P, D).transpose(1, 0, 2)),
        "c_t": f(np.asarray(L0_c).T), "wmod": f(L0_wmod),
        "q_const": q_const, "k_const": k_const, "tree": tree_matrices(),
        "ident": np.eye(P, dtype=np.float32),
    }
    nc = bacc.Bacc("TRN2", target_bir_lowering=False, num_devices=1)
    args = [nc.dram_tensor(f"in_{n}", a.shape, mybir.dt.from_np(a.dtype), kind="ExternalInput").ap()
            for n, a in arrays.items()]
    out = nc.dram_tensor("out", (B, S, D), F32, kind="ExternalOutput").ap()
    block_program(nc, *args, out)
    r = run_bass_kernel_spmd(nc, [{f"in_{n}": a for n, a in arrays.items()}], core_ids=[0])
    return r.results[0]["out"]
```
